# Optimizing a Trainium2 kernel written in Bass

```python
import numpy as np
import jax
import jax.numpy as jnp

def _softmax(x, axis=-1):
    return jax.nn.softmax(x, axis=axis)

def _gelu(x):
    return jax.nn.gelu(x, approximate=True)

def _silu(x):
    return jax.nn.silu(x)

def _sigmoid(x):
    return jax.nn.sigmoid(x)

def _layernorm(x, axis=-1, eps=1e-05):
    m = jnp.mean(x, axis=axis, keepdims=True)
    v = jnp.var(x, axis=axis, keepdims=True)
    return (x - m) / jnp.sqrt(v + eps)

def _scatter_add(tgt, idx, src, axis=0):
    return tgt.at[idx].add(src)

def _segment_sum(src, seg, n):
    return jax.ops.segment_sum(src, seg, n)
kernel_name = 'mk_xattn_seq_d1_seqx_r4_2f63df'

def setup_inputs(seed: int=0):
    np.random.seed(seed)
    _w = jnp.asarray

    def _rec_inputs():
        import jax
        import jax.numpy as jnp
        _rk = jax.random.key(seed)
        x = -0.0003929 + 0.9999 * jax.random.normal(jax.random.fold_in(_rk, 1), (8, 512, 256), jnp.float32)
        _lenS = 512 - jax.random.randint(jax.random.fold_in(_rk, 7), (8,), 0, max(1, 512 // 4) + 1, jnp.int32)
        _lenS2 = 512 - jax.random.randint(jax.random.fold_in(_rk, 8), (8,), 0, max(1, 512 // 4) + 1, jnp.int32)
        _ctx_1024P = jax.random.normal(jax.random.fold_in(_rk, 11), (8, 16, 256), jnp.float32)
        _ctx_1024c = jax.random.dirichlet(jax.random.fold_in(_rk, 511), 0.3 * jnp.ones((16,), jnp.float32), (8, 512))
        _ctx_1024t = jnp.einsum('bsk,bkd->bsd', _ctx_1024c, _ctx_1024P)
        _ctx_1024t = _ctx_1024t * jax.lax.rsqrt(jnp.mean(jnp.square(_ctx_1024t)) + 1e-12) * 0.953939
        ctx_1024 = 0.000227908 + 0.99994 * (_ctx_1024t + 0.3 * jax.random.normal(jax.random.fold_in(_rk, 611), (8, 512, 256), jnp.float32))
        itok_BxS_0_255 = jax.random.randint(jax.random.fold_in(_rk, 12), (8, 512), 0, 64, jnp.int32)
        return (x, ctx_1024, itok_BxS_0_255)
    x, ctx_1024, itok_BxS_0_255 = _rec_inputs()

    def _L0_xattn_setup():
        import jax, jax.numpy as jnp
        import numpy as np
        import math
        EPS_RMS = 1.1920929e-07
        EPS_DEN = 1e-06

        def rmsnorm(x, gamma):
            ms = jnp.mean(x * x, axis=-1, keepdims=True)
            return x * jax.lax.rsqrt(ms + EPS_RMS) * gamma
        key = jax.random.key(seed)
        ks = jax.random.split(key, 8)
        B, T, K, D = (4, 1024, 64, 256)
        x_tokens = jax.random.normal(ks[0], (B, T, D), dtype=jnp.float32)
        ctx = jax.random.normal(ks[1], (B, K, D), dtype=jnp.float32)
        idx = jnp.sort(jax.random.randint(ks[2], (B, T), 0, K), axis=-1)
        s = 1.0 / math.sqrt(D)
        Wq = jax.random.normal(ks[3], (D, D), dtype=jnp.float32) * s
        Wk = jax.random.normal(ks[4], (D, D), dtype=jnp.float32) * s
        Wv = jax.random.normal(ks[5], (D, D), dtype=jnp.float32) * s
        Wo = jax.random.normal(ks[6], (D, D), dtype=jnp.float32) * s
        return {'x_tokens': x_tokens, 'ctx': ctx, 'ctx_index_per_token': idx, 'gamma_q': jnp.ones((D,), jnp.float32), 'gamma_kv': jnp.ones((D,), jnp.float32), 'Wq': Wq, 'Wk': Wk, 'Wv': Wv, 'Wo': Wo}
    _L0_xattn_all = _L0_xattn_setup()
    _L0_xattn_in = {k: v for k, v in _L0_xattn_all.items() if k in ('gamma_q', 'gamma_kv', 'Wq', 'Wk', 'Wv', 'Wo')}
    del _L0_xattn_all
    return {'x': x, 'ctx_1024': ctx_1024, 'itok_BxS_0_255': itok_BxS_0_255, 'L0_xattn_gamma_q': _L0_xattn_in['gamma_q'], 'L0_xattn_gamma_kv': _L0_xattn_in['gamma_kv'], 'L0_xattn_Wq': _L0_xattn_in['Wq'], 'L0_xattn_Wk': _L0_xattn_in['Wk'], 'L0_xattn_Wv': _L0_xattn_in['Wv'], 'L0_xattn_Wo': _L0_xattn_in['Wo']}

def reference(x, ctx_1024, itok_BxS_0_255, L0_xattn_gamma_q, L0_xattn_gamma_kv, L0_xattn_Wq, L0_xattn_Wk, L0_xattn_Wv, L0_xattn_Wo):
    import jax
    import jax.numpy as jnp

    def _L0_xattn_ref(x_tokens, ctx, ctx_index_per_token, gamma_q, gamma_kv, Wq, Wk, Wv, Wo):
        import jax, jax.numpy as jnp
        import numpy as np
        import math
        EPS_RMS = 1.1920929e-07
        EPS_DEN = 1e-06

        def rmsnorm(x, gamma):
            ms = jnp.mean(x * x, axis=-1, keepdims=True)
            return x * jax.lax.rsqrt(ms + EPS_RMS) * gamma
        B, T, D = x_tokens.shape
        K = ctx.shape[1]
        H = 16
        hd = D // H

        def split(x):
            return x.reshape(B, -1, H, hd).transpose(0, 2, 1, 3)
        q = split(rmsnorm(x_tokens, gamma_q) @ Wq.T)
        kn = rmsnorm(ctx, gamma_kv)
        k = split(kn @ Wk.T)
        v = split(kn @ Wv.T)
        ctx_pos = jnp.arange(K)[None, None, :]
        mask = (jnp.abs(ctx_pos - ctx_index_per_token[:, :, None]) <= 1)[:, None]
        scores = jnp.einsum('bhqd,bhkd->bhqk', q, k) / math.sqrt(hd)
        w = jnp.square(jax.nn.relu(scores))
        w = jnp.where(mask, w, 0.0)
        denom = jnp.maximum(w.sum(-1, keepdims=True), EPS_DEN)
        out = jnp.einsum('bhqk,bhkd->bhqd', w / denom, v)
        out = out.transpose(0, 2, 1, 3).reshape(B, T, D)
        return x_tokens + out @ Wo.T
    x = _L0_xattn_ref(x, ctx_1024, itok_BxS_0_255, L0_xattn_gamma_q, L0_xattn_gamma_kv, L0_xattn_Wq, L0_xattn_Wk, L0_xattn_Wv, L0_xattn_Wo)
    return x

_drawn_inputs = setup_inputs


def setup_inputs(seed=0):
    import zlib

    import numpy as np

    out = dict(_drawn_inputs(seed))
    spreads = {'L0_xattn_gamma_q': (1.0, 0.2), 'L0_xattn_gamma_kv': (1.0, 0.2)}
    factors = {}
    for name, (base, spread) in spreads.items():
        noise = np.random.default_rng([zlib.crc32(name.encode()), seed]).standard_normal(out[name].shape)
        drawn = base * np.exp(spread * noise) if base else spread * noise
        out[name] = jnp.asarray(drawn.astype(out[name].dtype))
    for name, factor in factors.items():
        out[name] = (out[name] * factor).astype(out[name].dtype)
    return out
```

```python
from contextlib import ExitStack

import concourse.bass as bass
from concourse import mybir

F32 = mybir.dt.float32
F32R = mybir.dt.float32r
I32 = mybir.dt.int32
ALU = mybir.AluOpType
ACT = mybir.ActivationFunctionType
AX = mybir.AxisListType

B, S, D, H = 8, 512, 256, 16
HD = D // H
P = 128
KC = D // P
TPB = S // P
NT = B * TPB
WIN = 3
BLK = 64
ROWS = BLK + WIN - 1
NBLK = S // BLK + 2
EPS_RMS = 1.1920929e-07
EPS_DEN = 1e-06
T_LAG = 3
O_LAG = 4
R_LAG = 4


class Path:

    def __init__(self, blocks, ahead):
        self.blocks = blocks
        self.ahead = ahead

    def units(self, b):
        return [(b * len(self.blocks) + c, c) for c in range(len(self.blocks))]

    def slot(self, b, c):
        return b if self.ahead else c


NEAR = Path([0], 1)
ANY = Path(list(range(-1, NBLK - 1)), 0)


def wait_all(eng, *waits):
    for _, n in waits:
        if not isinstance(n, int):
            eng.compute_val(n)
    for sem, n in waits:
        eng.wait_ge(sem, n)


def over_batches(eng, body):
    body(0)
    with eng.Fori(1, B - 1) as b:
        body(b)
    body(B - 1)


def window_attention(nc, x_rows, x_cols, ctx_rows, ctx_cols, idx_cols, idx_all, gamma_q, gamma_kv, wq, wkv, wo, out):
    with ExitStack() as stack:
        def sb(name, shape, dt=F32):
            return stack.enter_context(nc.sbuf_tensor(name, shape, dt))

        def pb(name, shape):
            return stack.enter_context(nc.psum_tensor(name, shape, F32))

        def sem(name):
            return stack.enter_context(nc.semaphore(name))

        wq_raw = sb("wq_raw", [P, KC, D])
        wkv_raw = sb("wkv_raw", [P, KC, 2 * D])
        wq_sb = sb("wq_sb", [P, KC, D])
        wkv_sb = sb("wkv_sb", [P, KC, 2 * D])
        wo_sb = sb("wo_sb", [P, KC, D])
        gq_sb = sb("gq_sb", [P, KC])
        gkv_sb = sb("gkv_sb", [P, KC])
        ident = sb("ident", [P, P])
        ones = sb("ones", [P, P])
        idx_sb = sb("idx_sb", [P, NT], I32)
        idx_max = sb("idx_max", [P, 1])
        idx_min = sb("idx_min", [P, 1])
        above = sb("above", [P, 1])
        outside = sb("outside", [P, 1])
        path_flag = sb("path_flag", [1, 1], I32)
        x_sb = sb("x_sb", [P, NT, D])
        xT = sb("xT", [P, TPB, KC, P])
        idx_bc = sb("idx_bc", [P, B, S], I32)
        row_i32 = sb("row_i32", [P, 1], I32)
        row_and = sb("row_and", [P, 1], I32)
        row_of = sb("row_of", [P, 1])
        onehot = sb("onehot", [P, NBLK, S], F32R)
        cT = sb("cT", [P, KC, ROWS])
        c_rows = sb("c_rows", [ROWS, D])
        c_sq = sb("c_sq", [ROWS, D])
        c_ss = sb("c_ss", [ROWS, 1])
        c_var = sb("c_var", [ROWS, 1])
        c_root = sb("c_root", [ROWS, 1])
        c_r0 = sb("c_r0", [ROWS, 1])
        c_r0sq = sb("c_r0sq", [ROWS, 1])
        c_vr = sb("c_vr", [ROWS, 1])
        c_fix = sb("c_fix", [ROWS, 1])
        c_rms = sb("c_rms", [ROWS, 1])
        kv_hi = sb("kv_hi", [ROWS, 2 * D], F32R)
        kv_lo = sb("kv_lo", [ROWS, 2 * D], F32R)
        table = sb("table", [P, max(B, NBLK), WIN, 2 * D], F32R)
        x_sq = sb("x_sq", [P, D])
        x_ss = sb("x_ss", [P, TPB])
        den_eps = sb("den_eps", [P, TPB])
        q_sb = sb("q_sb", [P, 2, D])
        prod = sb("prod", [P, 2, WIN * D])
        score = sb("score", [P, TPB, WIN * H])
        w_raw = sb("w_raw", [P, 2, WIN * H])
        den = sb("den", [P, 2, H])
        den_max = sb("den_max", [P, 2, H])
        den_inv = sb("den_inv", [P, 2, H])
        w_sb = sb("w_sb", [P, TPB, WIN * H])
        v_sb = sb("v_sb", [P, TPB, WIN * D])
        wv = sb("wv", [P, 2, WIN * D])
        aT = sb("aT", [P, 2, KC, P])

        k_ps = pb("k_ps", [P, 2, 512])
        v_ps = pb("v_ps", [P, 2, 512])
        q_ps = pb("q_ps", [P, 512])
        a_ps = pb("a_ps", [P, 512])
        o_ps = pb("o_ps", [P, 512])
        kv_ps = pb("kv_ps", [P, 512])
        k_win = k_ps[:, :, :].rearrange("p a b -> p (a b)")
        v_win = v_ps[:, :, :].rearrange("p a b -> p (a b)")

        s_idx = sem("s_idx")
        s_weights = sem("s_weights")
        s_scaled = sem("s_scaled")
        s_const = sem("s_const")
        s_spread = sem("s_spread")
        s_outside = sem("s_outside")
        s_count = sem("s_count")
        s_flag = sem("s_flag")
        s_row = sem("s_row")
        xT_loaded = [sem(f"xT_loaded{i}") for i in range(TPB)]
        x_loaded = sem("x_loaded")
        idx_loaded = sem("idx_loaded")
        ctx_loaded = sem("ctx_loaded")
        ctx_squared = sem("ctx_squared")
        ctx_var = sem("ctx_var")
        ctx_root = sem("ctx_root")
        rms_step = sem("rms_step")
        ctx_rms = sem("ctx_rms")
        kv_ready = sem("kv_ready")
        hi_ready = sem("hi_ready")
        lo_ready = sem("lo_ready")
        table_loaded = sem("table_loaded")
        onehot_ready = sem("onehot_ready")
        x_squared = sem("x_squared")
        eps_ready = sem("eps_ready")
        q_ready = sem("q_ready")
        q_copied = sem("q_copied")
        k_ready = sem("k_ready")
        v_ready = sem("v_ready")
        v_copied = sem("v_copied")
        prod_ready = sem("prod_ready")
        score_ready = sem("score_ready")
        squared_ready = sem("squared_ready")
        den_step = sem("den_step")
        w_ready = sem("w_ready")
        wv_ready = sem("wv_ready")
        aT_ready = sem("aT_ready")
        aT_copied = sem("aT_copied")
        o_ready = sem("o_ready")
        res_ready = sem("res_ready")
        stored = sem("stored")

        block = stack.enter_context(nc.Block())

        def either(eng, run):
            eng.wait_ge(s_flag, 1)
            flag = eng.value_load(path_flag[0:1, 0:1], min_val=0, max_val=P)
            with eng.If(flag == 0):
                run(NEAR)
            with eng.Else():
                run(ANY)

        @block.sync
        def _(sp):
            sp.dma_start(idx_sb[:, :], idx_all).then_inc(s_idx, 16)
            for dst, src in ((wq_raw, wq), (wkv_raw, wkv), (wo_sb, wo)):
                sp.dma_start(dst[:, :, :], src).then_inc(s_weights, 16)
            for dst, src in ((gq_sb, gamma_q), (gkv_sb, gamma_kv)):
                sp.dma_start(dst[:, :], src).then_inc(s_weights, 16)

            def load_tokens(b):
                if not (isinstance(b, int) and b == 0):
                    sp.wait_ge(x_loaded, b * 16)
                    sp.wait_ge(idx_loaded, b * 16)
                sp.dma_start(x_sb[:, :, :].rearrange("p (b i) d -> p b i d", i=TPB)[:, b, :, :],
                             x_rows[b]).then_inc(x_loaded, 16)
                sp.dma_start(idx_bc[:, b, :], idx_cols[b].partition_broadcast(P)).then_inc(idx_loaded, 16)

            def load_columns(b, i):
                sp.dma_start(xT[:, i, :, :], x_cols[b, i]).then_inc(xT_loaded[i], 16)

            def load_context(path, b, u, c, first):
                if not first:
                    wait_all(sp, (kv_ready, u), (ctx_squared, u), (ctx_loaded, u * 32))
                sp.dma_start(cT[:, :, :], ctx_cols[b, path.blocks[c] + 1]).then_inc(ctx_loaded, 16)
                sp.dma_start(c_rows[:, :], ctx_rows[b, path.blocks[c] + 1]).then_inc(ctx_loaded, 16)

            def place_tables(path, b, u, c):
                if path.ahead or (isinstance(b, int) and b == 0):
                    sp.wait_ge(lo_ready, u + 1)
                else:
                    wait_all(sp, (lo_ready, u + 1), (v_ready, b * TPB))
                dst = table[:, path.slot(b, c), :, :]
                for j in range(WIN):
                    sp.dma_start(dst[0:BLK, j, :].bitcast(F32), kv_hi[j:j + BLK, :].bitcast(F32)).then_inc(table_loaded, 16)
                    sp.dma_start(dst[BLK:P, j, :].bitcast(F32), kv_lo[j:j + BLK, :].bitcast(F32)).then_inc(table_loaded, 16)

            def store(b, i):
                sp.wait_ge(res_ready, TPB * b + i + 2)
                rows = x_sb[:, :, :].rearrange("p (b i) d -> p b i d", i=TPB)
                sp.dma_start(out[b][:, i:i + 2, :], rows[:, b, i:i + 2, :]).then_inc(stored, 16)

            def run(path):
                load_context(path, 0, 0, 0, True)
                for i in range(TPB):
                    load_columns(0, i)
                load_tokens(0)
                if path.ahead:
                    place_tables(path, 0, 0, 0)

                def body(b):
                    first = isinstance(b, int) and b == 0
                    last = isinstance(b, int) and b == B - 1
                    if not path.ahead:
                        for u, c in path.units(b):
                            if not (first and c == 0):
                                load_context(path, b, u, c, False)
                            place_tables(path, b, u, c)
                    if not last:
                        if path.ahead:
                            load_context(path, b + 1, b + 1, 0, False)
                        load_tokens(b + 1)
                    for i in range(TPB):
                        if not last:
                            sp.wait_ge(q_ready, TPB * b + i + 1)
                            load_columns(b + 1, i)
                        if i == 1 and not first:
                            store(b - 1, 0)
                        if i == 2 and path.ahead and not last:
                            place_tables(path, b + 1, b + 1, 0)
                        if i == 3 and not first:
                            store(b - 1, 2)

                over_batches(sp, body)
                store(B - 1, 0)
                store(B - 1, 2)
                sp.wait_ge(stored, 16 * 2 * B)

            either(sp, run)

        @block.gpsimd
        def _(pool):
            nc.gpsimd.memset(ones[:, :], 1.0).then_inc(s_spread, 1)
            nc.gpsimd.iota(row_i32[:, :], pattern=[[0, 1]], base=0, channel_multiplier=1).then_inc(s_row, 1)
            pool.wait_ge(s_spread, 1)
            nc.gpsimd.affine_select(out=ident[:, :], in_=ones[:, :], compare_op=ALU.is_equal, fill=0.0, base=0,
                                    pattern=[[-1, P]], channel_multiplier=1).then_inc(s_const, 1)

            def run(path):
                def body(b):
                    first = isinstance(b, int) and b == 0
                    for i in range(TPB):
                        if i % 2 == 0:
                            pool.wait_ge(w_ready, (TPB * b + i) // 2 + 1 if isinstance(b, int) else b * 2 + i // 2 + 1)
                        pool.wait_ge(v_copied, TPB * b + i + 1)
                        if not first or i >= 2:
                            pool.wait_ge(aT_ready, TPB * b + i - 1)
                        nc.gpsimd.tensor_tensor(
                            wv[:, i % 2, :].rearrange("p (a d) -> p a d", d=HD),
                            v_sb[:, i, :].rearrange("p (a d) -> p a d", d=HD),
                            w_sb[:, i, :].unsqueeze(2).to_broadcast([P, WIN * H, HD]), ALU.mult).then_inc(wv_ready, 1)

                over_batches(pool, body)

            either(pool, run)

        @block.scalar
        def _(act):
            act.wait_ge(s_weights, 16 * 5)
            for k in range(KC):
                nc.scalar.activation(wkv_sb[:, k, :], wkv_raw[:, k, :], ACT.Copy, scale=gkv_sb[:, k:k + 1])
                last = nc.scalar.activation(wq_sb[:, k, :], wq_raw[:, k, :], ACT.Copy, scale=gq_sb[:, k:k + 1])
            last.then_inc(s_scaled, 1)

            def ctx_square(u):
                act.wait_ge(ctx_loaded, 32 * (u + 1))
                if not (isinstance(u, int) and u == 0):
                    act.wait_ge(ctx_var, u)
                nc.scalar.activation(c_sq[:, :], c_rows[:, :], ACT.Square, accum_out=c_ss[:, :]).then_inc(ctx_squared, 1)

            def ctx_sqrt(u):
                act.wait_ge(ctx_var, u + 1)
                nc.scalar.activation(c_root[:, :], c_var[:, :], ACT.Sqrt).then_inc(ctx_root, 1)

            def kv_high(u):
                act.wait_ge(kv_ready, u + 1)
                act.wait_ge(ctx_rms, u + 1)
                if not (isinstance(u, int) and u == 0):
                    act.wait_ge(table_loaded, u * 32 * WIN)
                nc.scalar.activation(kv_hi[:, :], kv_ps[0:ROWS, :], ACT.Copy, scale=c_rms[:, :]).then_inc(hi_ready, 1)

            def run(path):
                if path.ahead:
                    ctx_square(0)
                    ctx_sqrt(0)
                    kv_high(0)

                def copy_attention(t, i):
                    act.wait_ge(aT_ready, t + 1)
                    if not (isinstance(t, int) and t < 2):
                        act.wait_ge(o_ready, t - 1)
                    nc.scalar.activation(aT[:, i % 2, :, :].rearrange("p k t -> p (k t)"), a_ps[:, 0:D],
                                         ACT.Copy).then_inc(aT_copied, 1)

                def body(b):
                    first = isinstance(b, int) and b == 0
                    last = isinstance(b, int) and b == B - 1
                    if not path.ahead:
                        for u, _ in path.units(b):
                            ctx_square(u)
                            ctx_sqrt(u)
                            kv_high(u)
                    for i in range(TPB):
                        t = TPB * b + i
                        act.wait_ge(q_ready, t + 1)
                        if not first or i >= 2:
                            act.wait_ge(prod_ready, t - 1)
                        nc.scalar.activation(q_sb[:, i % 2, :], q_ps[:, 0:D], ACT.Copy).then_inc(q_copied, 1)
                        if i == 0:
                            act.wait_ge(x_loaded, 16 * (b + 1))
                        if not first or i > 0:
                            act.wait_ge(x_squared, t)
                        if not first:
                            act.wait_ge(eps_ready, 2 * b + i // 2 - 1)
                        nc.scalar.activation(x_sq[:, :], x_sb[:, t, :], ACT.Square,
                                             accum_out=x_ss[:, i:i + 1]).then_inc(x_squared, 1)
                        act.wait_ge(v_ready, t + 1)
                        if not first:
                            act.wait_ge(wv_ready, t - TPB + 1)
                        nc.scalar.activation(v_sb[:, i, :], v_win[:, 0:WIN * D], ACT.Copy).then_inc(v_copied, 1)
                        if not first or i >= T_LAG:
                            copy_attention(t - T_LAG, i - T_LAG)
                        if path.ahead and not last:
                            if i == 0:
                                ctx_square(b + 1)
                            if i == 1:
                                ctx_sqrt(b + 1)
                            if i == 2:
                                kv_high(b + 1)

                over_batches(act, body)
                for t in range(NT - T_LAG, NT):
                    copy_attention(t, t)

            either(act, run)

        @block.vector
        def _(dve):
            dve.wait_ge(s_idx, 16)
            nc.vector.tensor_reduce(idx_max[:, :], idx_sb[:, :], AX.X, ALU.max)
            nc.vector.tensor_reduce(idx_min[:, :], idx_sb[:, :], AX.X, ALU.min).then_inc(s_outside, 1)
            dve.wait_ge(s_outside, 1)
            nc.vector.tensor_scalar(above[:, :], idx_max[:, :], float(BLK - 1), None, ALU.is_gt).then_inc(s_outside, 1)
            dve.wait_ge(s_outside, 2)
            nc.vector.scalar_tensor_tensor(outside[:, :], idx_min[:, :], 0.0, above[:, :], ALU.is_lt,
                                           ALU.add).then_inc(s_outside, 1)
            dve.wait_ge(s_row, 1)
            nc.vector.tensor_scalar(row_and[:, :], row_i32[:, :], BLK - 1, None, ALU.bitwise_and).then_inc(s_row, 1)
            dve.wait_ge(s_row, 2)
            nc.vector.tensor_copy(row_of[:, :], row_and[:, :]).then_inc(s_row, 1)
            dve.wait_ge(s_count, 1)
            nc.vector.tensor_copy(path_flag[0:1, 0:1], q_ps[0:1, 0:1]).then_inc(s_flag, 1)
            dve.wait_ge(s_row, 3)

            def kv_variance(u):
                dve.wait_ge(ctx_squared, u + 1)
                if not (isinstance(u, int) and u == 0):
                    dve.wait_ge(ctx_root, u)
                nc.vector.tensor_scalar(c_var[:, :], c_ss[:, :], 1.0 / D, EPS_RMS, ALU.mult, ALU.add).then_inc(ctx_var, 1)

            def kv_rsqrt(u):
                dve.wait_ge(ctx_root, u + 1)
                nc.vector.reciprocal(c_r0[:, :], c_root[:, :]).then_inc(rms_step, 1)
                dve.wait_ge(rms_step, 4 * u + 1)
                nc.vector.tensor_tensor(c_r0sq[:, :], c_r0[:, :], c_r0[:, :], ALU.mult).then_inc(rms_step, 1)
                dve.wait_ge(rms_step, 4 * u + 2)
                nc.vector.tensor_tensor(c_vr[:, :], c_r0sq[:, :], c_var[:, :], ALU.mult).then_inc(rms_step, 1)
                dve.wait_ge(rms_step, 4 * u + 3)
                nc.vector.tensor_scalar(c_fix[:, :], c_vr[:, :], -0.5, 1.5, ALU.mult, ALU.add).then_inc(rms_step, 1)
                dve.wait_ge(rms_step, 4 * u + 4)
                if not (isinstance(u, int) and u == 0):
                    dve.wait_ge(lo_ready, u)
                nc.vector.tensor_tensor(c_rms[:, :], c_r0[:, :], c_fix[:, :], ALU.mult).then_inc(ctx_rms, 1)

            def kv_low(u):
                dve.wait_ge(hi_ready, u + 1)
                nc.vector.scalar_tensor_tensor(kv_lo[:, :], kv_ps[0:ROWS, :], c_rms[:, :], kv_hi[:, :].bitcast(F32),
                                               ALU.mult, ALU.subtract).then_inc(lo_ready, 1)

            idx_tiles = idx_bc[:, :, :].rearrange("p b (i t) -> p (b i) t", t=P)

            def make_onehot(path, t, i):
                for c, blk in enumerate(path.blocks):
                    last = nc.vector.tensor_scalar(onehot[:, c, i * P:(i + 1) * P], idx_tiles[:, t, :], float(BLK * blk),
                                                   row_of[:, :], ALU.subtract, ALU.is_equal)
                last.then_inc(onehot_ready, 1)

            def residual(t):
                dve.wait_ge(o_ready, t + 1)
                nc.vector.tensor_tensor(x_sb[:, t, :], o_ps[:, 0:D], x_sb[:, t, :], ALU.add).then_inc(res_ready, 1)

            def run(path):
                dve.wait_ge(idx_loaded, 16)
                make_onehot(path, 0, 0)
                make_onehot(path, 1, 1)
                if path.ahead:
                    kv_variance(0)
                    kv_rsqrt(0)
                    kv_low(0)

                def weights(b, i):
                    pair = 2 * b + i // 2
                    both = slice(i - 1, i + 1)
                    dve.wait_ge(x_squared, TPB * b + i + 1)
                    nc.vector.tensor_scalar(den_eps[:, both], x_ss[:, both], HD * EPS_DEN / D, HD * EPS_DEN * EPS_RMS,
                                            ALU.mult, ALU.add).then_inc(eps_ready, 1)
                    dve.wait_ge(score_ready, TPB * b + i + 1)
                    nc.vector.scalar_tensor_tensor(w_raw[:, :, :], score[:, both, :], 0.0, score[:, both, :],
                                                   ALU.max, ALU.mult).then_inc(squared_ready, 1)
                    dve.wait_ge(squared_ready, pair + 1)
                    nc.vector.tensor_reduce(den[:, :, :], w_raw[:, :, :].rearrange("p t (j h) -> p t h j", j=WIN),
                                            AX.X, ALU.add).then_inc(den_step, 1)
                    dve.wait_ge(den_step, 3 * pair + 1)
                    dve.wait_ge(eps_ready, pair + 1)
                    nc.vector.tensor_tensor(den_max[:, :, :], den[:, :, :],
                                            den_eps[:, both].unsqueeze(2).to_broadcast([P, 2, H]),
                                            ALU.max).then_inc(den_step, 1)
                    dve.wait_ge(den_step, 3 * pair + 2)
                    nc.vector.reciprocal(den_inv[:, :, :], den_max[:, :, :]).then_inc(den_step, 1)
                    dve.wait_ge(den_step, 3 * pair + 3)
                    if not (isinstance(b, int) and b == 0):
                        dve.wait_ge(wv_ready, TPB * b + i - TPB + 1)
                    for k in range(2):
                        last = nc.vector.tensor_tensor(
                            w_sb[:, i - 1 + k, :].rearrange("p (j h) -> p j h", j=WIN),
                            w_raw[:, k, :].rearrange("p (j h) -> p j h", j=WIN),
                            den_inv[:, k, :].unsqueeze(1).to_broadcast([P, WIN, H]), ALU.mult)
                    last.then_inc(w_ready, 1)

                def body(b):
                    first = isinstance(b, int) and b == 0
                    last = isinstance(b, int) and b == B - 1
                    if not path.ahead:
                        for u, _ in path.units(b):
                            kv_variance(u)
                            kv_rsqrt(u)
                            kv_low(u)
                    for i in range(TPB):
                        t = TPB * b + i
                        if not (last and i >= 2):
                            if i == 2:
                                dve.wait_ge(idx_loaded, 16 * (b + 2))
                            if not first or i >= 2:
                                dve.wait_ge(v_ready, t - 1)
                            make_onehot(path, t + 2, (i + 2) % TPB)
                        dve.wait_ge(q_copied, t + 1)
                        dve.wait_ge(k_ready, t + 1)
                        nc.vector.tensor_tensor(
                            prod[:, i % 2, :].rearrange("p (j d) -> p j d", j=WIN),
                            k_win[:, 0:WIN * D].rearrange("p (j d) -> p j d", j=WIN),
                            q_sb[:, i % 2, :].unsqueeze(1).to_broadcast([P, WIN, D]), ALU.mult).then_inc(prod_ready, 1)
                        dve.wait_ge(prod_ready, t + 1)
                        nc.vector.tensor_reduce(score[:, i, :], prod[:, i % 2, :].rearrange("p (a d) -> p a d", d=HD),
                                                AX.X, ALU.add).then_inc(score_ready, 1)
                        if i % 2 == 1:
                            weights(b, i)
                        if not first:
                            residual(t - R_LAG)
                        if path.ahead and not last:
                            if i == 0:
                                kv_variance(b + 1)
                            if i == 1:
                                kv_rsqrt(b + 1)
                            if i == 2:
                                kv_low(b + 1)

                over_batches(dve, body)
                for t in range(NT - R_LAG, NT):
                    residual(t)

            either(dve, run)

        @block.tensor
        def _(pe):
            pe.wait_ge(s_outside, 3)
            pe.wait_ge(s_spread, 1)
            nc.tensor.matmul(q_ps[0:1, 0:1], outside[:, :], ones[:, 0:1], start=True, stop=True).then_inc(s_count, 1)
            pe.wait_ge(s_const, 1)
            pe.wait_ge(s_weights, 16 * 5)
            pe.wait_ge(s_scaled, 1)

            def kv_project(u):
                pe.wait_ge(ctx_loaded, 32 * (u + 1))
                if not (isinstance(u, int) and u == 0):
                    pe.wait_ge(lo_ready, u)
                for k in range(KC):
                    last = nc.tensor.matmul(kv_ps[0:ROWS, :], cT[:, k, :], wkv_sb[:, k, :], start=(k == 0), stop=(k == KC - 1))
                last.then_inc(kv_ready, 1)

            def gather(path, b, i, to, at, done):
                n = len(path.blocks)
                for j in range(WIN):
                    for c in range(n):
                        last = nc.tensor.matmul(to[:, j * D:(j + 1) * D], onehot[:, c, i * P:(i + 1) * P],
                                                table[:, path.slot(b, c), j, at:at + D], start=(c == 0), stop=(c == n - 1))
                last.then_inc(done, 1)

            def transpose_sum(t, i):
                pe.wait_ge(wv_ready, t + 1)
                if not (isinstance(t, int) and t == 0):
                    pe.wait_ge(aT_copied, t)
                for k in range(KC):
                    for j in range(WIN):
                        last = nc.tensor.matmul(a_ps[:, k * P:(k + 1) * P], wv[:, i % 2, j * D + k * P:j * D + (k + 1) * P],
                                                ident[:, :], start=(j == 0), stop=(j == WIN - 1), is_transpose=True)
                last.then_inc(aT_ready, 1)

            def project_out(t, i):
                pe.wait_ge(aT_copied, t + 1)
                if not (isinstance(t, int) and t == 0):
                    pe.wait_ge(res_ready, t)
                for k in range(KC):
                    last = nc.tensor.matmul(o_ps[:, 0:D], aT[:, i % 2, k, :], wo_sb[:, k, :], start=(k == 0), stop=(k == KC - 1))
                last.then_inc(o_ready, 1)

            def run(path):
                if path.ahead:
                    kv_project(0)

                def body(b):
                    first = isinstance(b, int) and b == 0
                    last = isinstance(b, int) and b == B - 1
                    if not path.ahead:
                        for u, _ in path.units(b):
                            kv_project(u)
                    for i in range(TPB):
                        t = TPB * b + i
                        pe.wait_ge(xT_loaded[i], 16 * (b + 1))
                        if not (first and i == 0):
                            pe.wait_ge(q_copied, t)
                        for k in range(KC):
                            mm = nc.tensor.matmul(q_ps[:, 0:D], xT[:, i, k, :], wq_sb[:, k, :], start=(k == 0), stop=(k == KC - 1))
                        mm.then_inc(q_ready, 1)
                        if i == 0:
                            pe.wait_ge(table_loaded, 32 * WIN * len(path.blocks) * (b + 1))
                        pe.wait_ge(onehot_ready, t + 1)
                        if not (first and i == 0):
                            pe.wait_ge(prod_ready, t)
                        gather(path, b, i, k_win, 0, k_ready)
                        if not first or i >= O_LAG:
                            project_out(t - O_LAG, i - O_LAG)
                        if not first or i >= T_LAG:
                            transpose_sum(t - T_LAG, i - T_LAG)
                        if not (first and i == 0):
                            pe.wait_ge(v_copied, t)
                        gather(path, b, i, v_win, D, v_ready)
                        if path.ahead and not last and i == 1:
                            kv_project(b + 1)

                over_batches(pe, body)
                for t in range(NT - O_LAG, NT):
                    if t >= NT - O_LAG + 1:
                        transpose_sum(t, t)
                    project_out(t, t)

            either(pe, run)


def kernel(x, ctx_1024, itok_BxS_0_255, L0_xattn_gamma_q, L0_xattn_gamma_kv, L0_xattn_Wq, L0_xattn_Wk, L0_xattn_Wv,
           L0_xattn_Wo):
    import numpy as np
    import concourse.bacc as bacc
    from concourse.bass_utils import run_bass_kernel_spmd

    x, ctx, idx = np.asarray(x), np.asarray(ctx_1024), np.asarray(itok_BxS_0_255)
    wq, wk, wv, wo = (np.asarray(w) for w in (L0_xattn_Wq, L0_xattn_Wk, L0_xattn_Wv, L0_xattn_Wo))
    gq, gkv = np.asarray(L0_xattn_gamma_q), np.asarray(L0_xattn_gamma_kv)

    def chunked(a):
        return np.ascontiguousarray(a.reshape(KC, P, -1).transpose(1, 0, 2))

    x_rows = x.reshape(B, P, TPB, D)
    x_cols = x_rows.reshape(B, P, TPB, KC, P).transpose(0, 2, 4, 3, 1)
    idx_cols = idx.reshape(B, P, TPB).transpose(0, 2, 1).reshape(B, S)
    pad = np.zeros((B, BLK + 1, D), ctx.dtype)
    padded = np.concatenate([pad, ctx, pad], axis=1)
    blocks = np.stack([padded[:, c * BLK:c * BLK + ROWS] for c in range(NBLK)], axis=1)
    ctx_cols = blocks.reshape(B, NBLK, ROWS, KC, P).transpose(0, 1, 4, 3, 2)

    arrays = {
        "x_rows": x_rows, "x_cols": x_cols, "ctx_rows": blocks, "ctx_cols": ctx_cols, "idx_cols": idx_cols,
        "idx_all": idx.reshape(P, NT), "gamma_q": gq.reshape(KC, P).T, "gamma_kv": gkv.reshape(KC, P).T,
        "wq": chunked(wq.T), "wkv": chunked(np.concatenate([wk.T, wv.T], axis=1)), "wo": chunked(wo.T),
    }
    arrays = {n: np.ascontiguousarray(a) for n, a in arrays.items()}
    nc = bacc.Bacc("TRN2", target_bir_lowering=False, num_devices=1)
    aps = {n: nc.dram_tensor(n, a.shape, mybir.dt.from_np(a.dtype), kind="ExternalInput").ap() for n, a in arrays.items()}
    out = nc.dram_tensor("out", (B, P, TPB, D), F32, kind="ExternalOutput").ap()
    window_attention(nc, **aps, out=out)
    r = run_bass_kernel_spmd(nc, [arrays], core_ids=[0])
    return r.results[0]["out"].reshape(B, S, D)
```

```python
from contextlib import ExitStack

import concourse.bass as bass
from concourse import mybir

F32 = mybir.dt.float32
F32R = mybir.dt.float32r
I32 = mybir.dt.int32
ALU = mybir.AluOpType
ACT = mybir.ActivationFunctionType
AX = mybir.AxisListType

B, S, D, H = 8, 512, 256, 16
HD = D // H
P = 128
KC = D // P
TPB = S // P
NT = B * TPB
WIN = 3
BLK = 64
ROWS = BLK + WIN - 1
NBLK = S // BLK + 2
EPS_RMS = 1.1920929e-07
EPS_DEN = 1e-06
SQ_SCALE = (HD * EPS_DEN / D) ** 0.5
DEN_LEAST = HD * EPS_DEN * EPS_RMS
LAG = TPB
PARTS = ((0, 0), (0, 1), (1, 0))


class Path:

    def __init__(self, blocks, ahead):
        self.blocks = blocks
        self.ahead = ahead

    def units(self, b):
        if self.ahead:
            return [(b, b)]
        return [(b * len(self.blocks) + c, c) for c in range(len(self.blocks))]


NEAR = Path([0], True)
ANY = Path(list(range(-1, NBLK - 1)), False)


def is_first(n):
    return isinstance(n, int) and n == 0


def is_last(b):
    return isinstance(b, int) and b == B - 1


def first_tile(b, i):
    return is_first(b) and i == 0


def wait_all(eng, *waits):
    for _, n in waits:
        if not isinstance(n, int):
            eng.compute_val(n)
    for sem, n in waits:
        eng.wait_ge(sem, n)


def over_batches(eng, body):
    body(0)
    with eng.Fori(1, B - 1) as b:
        body(b)
    body(B - 1)


def window_attention(nc, x_rows, x_cols, ctx_rows, ctx_cols, idx_cols, idx_all, gamma_q, gamma_kv, wq, wkv, wo, out):
    with ExitStack() as stack:
        def sb(name, shape, dt=F32):
            return stack.enter_context(nc.sbuf_tensor(name, shape, dt))

        def pb(name, shape):
            return stack.enter_context(nc.psum_tensor(name, shape, F32))

        def sem(name):
            return stack.enter_context(nc.semaphore(name))

        wkv_raw = sb("wkv_raw", [P, KC, 2 * D])
        wo_raw = sb("wo_raw", [P, KC, D])
        wq_hl = sb("wq_hl", [P, 2, KC, D], F32R)
        wkv_hl = sb("wkv_hl", [P, 2, KC, 2 * D], F32R)
        wo_hl = sb("wo_hl", [P, 2, KC, D], F32R)
        gq_sb = sb("gq_sb", [P, KC])
        gkv_sb = sb("gkv_sb", [P, KC])
        ident = sb("ident", [P, P])
        ones = sb("ones", [P, P])
        idx_sb = sb("idx_sb", [P, NT], I32)
        idx_max = sb("idx_max", [P, 1])
        idx_min = sb("idx_min", [P, 1])
        above = sb("above", [P, 1])
        outside = sb("outside", [P, 1])
        path_flag = sb("path_flag", [1, 1], I32)
        x_sb = sb("x_sb", [P, NT, D])
        xT = sb("xT", [P, TPB, KC, P])
        xT_hl = sb("xT_hl", [P, TPB, 2, KC, P], F32R)
        idx_bc = sb("idx_bc", [P, B, S], I32)
        row_i32 = sb("row_i32", [P, 1], I32)
        row_and = sb("row_and", [P, 1], I32)
        row_of = sb("row_of", [P, 1])
        onehot = sb("onehot", [P, NBLK, P], F32R)
        cT = sb("cT", [P, NBLK, KC * ROWS])
        cT_hl = sb("cT_hl", [P, 2, KC, ROWS], F32R)
        c_rows = sb("c_rows", [ROWS, NBLK, D])
        c_sq = sb("c_sq", [ROWS, D])
        c_ss = sb("c_ss", [ROWS, NBLK])
        c_var = sb("c_var", [ROWS, NBLK])
        c_root = sb("c_root", [ROWS, NBLK])
        c_r0 = sb("c_r0", [ROWS, NBLK])
        c_r0sq = sb("c_r0sq", [ROWS, NBLK])
        c_vr = sb("c_vr", [ROWS, NBLK])
        c_fix = sb("c_fix", [ROWS, NBLK])
        c_rms = sb("c_rms", [ROWS, NBLK])
        kv_hi = sb("kv_hi", [ROWS, 2 * D], F32R)
        kv_lo = sb("kv_lo", [ROWS, 2 * D], F32R)
        table = sb("table", [P, max(B, NBLK), WIN, 2 * D], F32R)
        x_sq = sb("x_sq", [P, D])
        x_ss = sb("x_ss", [P, TPB])
        q_sb = sb("q_sb", [P, 2, D])
        prod = sb("prod", [P, 2, WIN * D])
        score = sb("score", [P, TPB, WIN * H])
        w_raw = sb("w_raw", [P, 2, WIN * H])
        den = sb("den", [P, 2, H])
        den_max = sb("den_max", [P, 2, H])
        den_inv = sb("den_inv", [P, 2, H])
        w_sb = sb("w_sb", [P, TPB, WIN * H])
        v_sb = sb("v_sb", [P, TPB, WIN * D])
        wq_raw = v_sb[:, TPB - 1, 0:KC * D].rearrange("p (k n) -> p k n", k=KC)
        wv = sb("wv", [P, 2, WIN * D])
        aT_hl = sb("aT_hl", [P, 2, 2, KC, P], F32R)
        o_sb = sb("o_sb", [P, TPB, D])

        k_ps = pb("k_ps", [P, 2, 512])
        v_ps = pb("v_ps", [P, 2, 512])
        q_ps = pb("q_ps", [P, 512])
        a_ps = pb("a_ps", [P, 512])
        o_ps = pb("o_ps", [P, 512])
        kv_ps = pb("kv_ps", [P, 512])
        k_win = k_ps[:, :, :].rearrange("p a b -> p (a b)")
        v_win = v_ps[:, :, :].rearrange("p a b -> p (a b)")

        idx_here = sem("idx_here")
        wkv_here = sem("wkv_here")
        wq_here = sem("wq_here")
        wo_here = sem("wo_here")
        wkv_high = sem("wkv_high")
        wkv_split = sem("wkv_split")
        wq_high = sem("wq_high")
        wq_split = sem("wq_split")
        wo_high = sem("wo_high")
        wo_split = sem("wo_split")
        ones_ready = sem("ones_ready")
        ident_ready = sem("ident_ready")
        outside_step = sem("outside_step")
        outside_summed = sem("outside_summed")
        flag_ready = sem("flag_ready")
        row_step = sem("row_step")
        xT_loaded = [sem(f"xT_loaded{i}") for i in range(TPB)]
        xT_high = sem("xT_high")
        xT_split = sem("xT_split")
        x_loaded = sem("x_loaded")
        idx_loaded = sem("idx_loaded")
        ctx_loaded = sem("ctx_loaded")
        ctx_squared = sem("ctx_squared")
        ctx_var = sem("ctx_var")
        ctx_root = sem("ctx_root")
        rms_step = sem("rms_step")
        ctx_rms = sem("ctx_rms")
        cT_high = sem("cT_high")
        cT_split = sem("cT_split")
        kv_ready = sem("kv_ready")
        hi_ready = sem("hi_ready")
        lo_ready = sem("lo_ready")
        table_loaded = sem("table_loaded")
        onehot_ready = sem("onehot_ready")
        x_squared = sem("x_squared")
        q_ready = sem("q_ready")
        q_copied = sem("q_copied")
        k_ready = sem("k_ready")
        v_ready = sem("v_ready")
        v_copied = sem("v_copied")
        prod_ready = sem("prod_ready")
        score_ready = sem("score_ready")
        squared_ready = sem("squared_ready")
        den_step = sem("den_step")
        w_ready = sem("w_ready")
        wv_ready = sem("wv_ready")
        aT_ready = sem("aT_ready")
        aT_high = sem("aT_high")
        aT_split = sem("aT_split")
        o_ready = sem("o_ready")
        o_copied = sem("o_copied")
        res_ready = sem("res_ready")
        stored = sem("stored")

        block = stack.enter_context(nc.Block())

        def either(eng, run):
            eng.wait_ge(flag_ready, 1)
            flag = eng.value_load(path_flag[0:1, 0:1], min_val=0, max_val=P)
            with eng.If(flag == 0):
                run(NEAR)
            with eng.Else():
                run(ANY)

        @block.sync
        def _(sp):
            def load_columns(b, i):
                sp.dma_start(xT[:, i, :, :], x_cols[b, i]).then_inc(xT_loaded[i], 16)

            def load_tokens(b):
                if not is_first(b):
                    sp.wait_ge(x_loaded, b * 16)
                    sp.wait_ge(idx_loaded, b * 16)
                sp.dma_start(idx_bc[:, b, :], idx_cols[b].partition_broadcast(P)).then_inc(idx_loaded, 16)
                sp.dma_start(x_sb[:, :, :].rearrange("p (b i) d -> p b i d", i=TPB)[:, b, :, :],
                             x_rows[b]).then_inc(x_loaded, 16)

            sp.dma_start(idx_sb[:, :], idx_all).then_inc(idx_here, 16)
            sp.dma_start(c_rows[:, 0:B, :], ctx_rows[:, 1].rearrange("b r d -> r b d")).then_inc(ctx_loaded, 16)
            sp.dma_start(gkv_sb[:, :], gamma_kv).then_inc(wkv_here, 16)
            sp.dma_start(wkv_raw[:, :, :], wkv).then_inc(wkv_here, 16)
            sp.dma_start(cT[:, 0:B, :], ctx_cols[:, 1].rearrange("b p k r -> p b (k r)")).then_inc(ctx_loaded, 16)
            load_columns(0, 0)
            sp.dma_start(gq_sb[:, :], gamma_q).then_inc(wq_here, 16)
            sp.dma_start(wq_raw[:, :, :], wq).then_inc(wq_here, 16)
            load_tokens(0)
            for i in range(1, TPB):
                load_columns(0, i)
            sp.dma_start(wo_raw[:, :, :], wo).then_inc(wo_here, 16)

            def load_context(b):
                if not is_first(b):
                    sp.wait_ge(cT_split, b * NBLK)
                sp.wait_ge(ctx_loaded, (b + 1) * 32)
                sp.wait_ge(ctx_squared, b * NBLK) if not is_first(b) else None
                sp.dma_start(c_rows[:, :, :], ctx_rows[b].rearrange("c r d -> r c d")).then_inc(ctx_loaded, 16)
                sp.dma_start(cT[:, :, :], ctx_cols[b].rearrange("c p k r -> p c (k r)")).then_inc(ctx_loaded, 16)

            def place_table(u, slot, tiles=None):
                if tiles is None:
                    sp.wait_ge(lo_ready, u + 1)
                else:
                    wait_all(sp, (v_ready, tiles), (lo_ready, u + 1))
                dst = table[:, slot, :, :]
                for j in range(WIN):
                    sp.dma_start(dst[0:BLK, j, :].bitcast(F32), kv_hi[j:j + BLK, :].bitcast(F32)).then_inc(table_loaded, 16)
                    sp.dma_start(dst[BLK:P, j, :].bitcast(F32), kv_lo[j:j + BLK, :].bitcast(F32)).then_inc(table_loaded, 16)

            def store(b, i):
                sp.wait_ge(res_ready, TPB * b + i + 2)
                rows = x_sb[:, :, :].rearrange("p (b i) d -> p b i d", i=TPB)
                sp.dma_start(out[b][:, i:i + 2, :], rows[:, b, i:i + 2, :]).then_inc(stored, 16)

            def run(path):
                if path.ahead:
                    place_table(0, 0)

                def body(b):
                    if not path.ahead:
                        load_context(b)
                        for u, slot in path.units(b):
                            place_table(u, slot, TPB * b if slot == 0 and not is_first(b) else None)
                    if not is_last(b):
                        load_tokens(b + 1)
                    for i in range(TPB):
                        if i == 1 and not is_first(b):
                            store(b - 1, 0)
                        if i == 3 and not is_first(b):
                            store(b - 1, 2)
                        if not is_last(b):
                            sp.wait_ge(xT_split, TPB * b + i + 1)
                            load_columns(b + 1, i)
                            if i == 1 and path.ahead:
                                place_table(b + 1, b + 1)

                over_batches(sp, body)
                store(B - 1, 0)
                store(B - 1, 2)
                sp.wait_ge(stored, 16 * 2 * B)

            either(sp, run)

        @block.gpsimd
        def _(pool):
            nc.gpsimd.memset(ones[:, :], 1.0).then_inc(ones_ready, 1)
            nc.gpsimd.iota(row_i32[:, :], pattern=[[0, 1]], base=0, channel_multiplier=1).then_inc(row_step, 1)
            pool.wait_ge(ones_ready, 1)
            nc.gpsimd.affine_select(out=ident[:, :], in_=ones[:, :], compare_op=ALU.is_equal, fill=0.0, base=0,
                                    pattern=[[-1, P]], channel_multiplier=1).then_inc(ident_ready, 1)

            def split_columns(t, i):
                pool.wait_ge(xT_high, t + 1)
                nc.gpsimd.tensor_tensor(xT_hl[:, i, 1, :, :], xT[:, i, :, :], xT_hl[:, i, 0, :, :].bitcast(F32),
                                        ALU.subtract).then_inc(xT_split, 1)

            def residual(t, i):
                pool.wait_ge(o_copied, t + 1)
                nc.gpsimd.tensor_tensor(x_sb[:, t, :], o_sb[:, i % TPB, :], x_sb[:, t, :], ALU.add).then_inc(res_ready, 1)

            def run(path):
                split_columns(0, 0)
                split_columns(1, 1)
                pool.wait_ge(wo_here, 16)
                nc.gpsimd.tensor_copy(wo_hl[:, 0, :, :], wo_raw[:, :, :]).then_inc(wo_high, 1)
                pool.wait_ge(wo_high, 1)
                nc.gpsimd.tensor_tensor(wo_hl[:, 1, :, :], wo_raw[:, :, :], wo_hl[:, 0, :, :].bitcast(F32),
                                        ALU.subtract).then_inc(wo_split, 1)
                for i in range(2, TPB):
                    split_columns(i, i)

                def body(b):
                    for i in range(TPB):
                        t = TPB * b + i
                        if not is_first(b) or i >= 2:
                            residual(t - 2, (i - 2) % TPB)
                        if not is_last(b):
                            split_columns(t + TPB, i)
                        pool.wait_ge(w_ready, 2 * b + i // 2 + 1)
                        pool.wait_ge(v_copied, t + 1)
                        if not is_first(b) or i >= 2:
                            pool.wait_ge(aT_ready, t - 1)
                        nc.gpsimd.tensor_tensor(
                            wv[:, i % 2, :].rearrange("p (a d) -> p a d", d=HD),
                            v_sb[:, i, :].rearrange("p (a d) -> p a d", d=HD),
                            w_sb[:, i, :].unsqueeze(2).to_broadcast([P, WIN * H, HD]), ALU.mult).then_inc(wv_ready, 1)

                over_batches(pool, body)
                residual(NT - 2, 2)
                residual(NT - 1, 3)

            either(pool, run)

        @block.scalar
        def _(act):
            act.wait_ge(ones_ready, 1)
            nc.scalar.activation(c_root[0:1, 0:1], ones[0:1, 0:1], ACT.Sqrt)

            def ctx_square(u, slot, loads):
                act.wait_ge(ctx_loaded, loads)
                if not is_first(u):
                    act.wait_ge(ctx_squared, u)
                nc.scalar.activation(c_sq[:, :], c_rows[:, slot, :], ACT.Square,
                                     accum_out=c_ss[:, :].unsqueeze(2)[:, slot, :]).then_inc(ctx_squared, 1)

            def ctx_sqrt(g, slots):
                act.wait_ge(ctx_var, g + 1)
                nc.scalar.activation(c_root[:, slots], c_var[:, slots], ACT.Sqrt).then_inc(ctx_root, 1)

            def ctx_high(u, slot):
                if is_first(u):
                    act.wait_ge(ctx_loaded, 32)
                else:
                    act.wait_ge(kv_ready, u)
                nc.scalar.activation(cT_hl[:, 0, :, :].rearrange("p k r -> p (k r)"), cT[:, slot, :],
                                     ACT.Copy).then_inc(cT_high, 1)

            def kv_high(g, u, slot):
                act.wait_ge(kv_ready, u + 1)
                act.wait_ge(ctx_rms, g + 1)
                if not is_first(u):
                    act.wait_ge(table_loaded, u * 32 * WIN)
                nc.scalar.activation(kv_hi[:, :], kv_ps[0:ROWS, :], ACT.Copy,
                                     scale=c_rms[:, :].unsqueeze(2)[:, slot, :]).then_inc(hi_ready, 1)

            def columns_high(t, i, loads):
                act.wait_ge(xT_loaded[i], loads)
                nc.scalar.activation(xT_hl[:, i, 0, :, :], xT[:, i, :, :], ACT.Copy).then_inc(xT_high, 1)

            def attention_high(t, i):
                act.wait_ge(aT_ready, t + 1)
                nc.scalar.activation(aT_hl[:, i % 2, 0, :, :].rearrange("p k t -> p (k t)"), a_ps[:, 0:D],
                                     ACT.Copy).then_inc(aT_high, 1)

            def copy_out(t, i):
                act.wait_ge(o_ready, t + 1)
                nc.scalar.activation(o_sb[:, i % TPB, :], o_ps[:, 0:D], ACT.Copy).then_inc(o_copied, 1)

            def run(path):
                act.wait_ge(wkv_here, 32)
                for k in range(KC):
                    last = nc.scalar.activation(wkv_hl[:, 0, k, :], wkv_raw[:, k, :], ACT.Copy, scale=gkv_sb[:, k:k + 1])
                last.then_inc(wkv_high, 1)
                if path.ahead:
                    ctx_high(0, 0)
                    ctx_square(0, 0, 32)
                    ctx_sqrt(0, slice(0, 1))
                act.wait_ge(wq_here, 32)
                for k in range(KC):
                    last = nc.scalar.activation(wq_hl[:, 0, k, :], wq_raw[:, k, :], ACT.Copy, scale=gq_sb[:, k:k + 1])
                last.then_inc(wq_high, 1)
                columns_high(0, 0, 16)
                if path.ahead:
                    kv_high(0, 0, 0)
                columns_high(1, 1, 16)
                if path.ahead:
                    for u in range(1, B):
                        ctx_square(u, u, 32)
                    ctx_sqrt(1, slice(1, B))

                def body(b):
                    if not path.ahead:
                        for u, slot in path.units(b):
                            ctx_square(u, slot, 32 * (b + 2))
                        ctx_sqrt(b, slice(0, NBLK))
                        for u, slot in path.units(b):
                            ctx_high(u, slot)
                            kv_high(b, u, slot)
                    for i in range(TPB):
                        t = TPB * b + i
                        if not is_first(b):
                            attention_high(t - LAG, i)
                        if path.ahead and not is_last(b) and i == 0:
                            ctx_high(b + 1, b + 1)
                        act.wait_ge(q_ready, t + 1)
                        if not is_first(b) or i >= 2:
                            act.wait_ge(prod_ready, t - 1)
                        nc.scalar.activation(q_sb[:, i % 2, :], q_ps[:, 0:D], ACT.Copy).then_inc(q_copied, 1)
                        if i < 2:
                            if not is_first(b):
                                act.wait_ge(q_ready, t - 1)
                            columns_high(t + 2, i + 2, 16 * (b + 1))
                        elif not is_last(b):
                            act.wait_ge(q_ready, t - 1)
                            columns_high(t + 2, i - 2, 16 * (b + 2))
                        if path.ahead and not is_last(b) and i == 1:
                            kv_high(1, b + 1, b + 1)
                        act.wait_ge(v_ready, t + 1)
                        if not is_first(b):
                            act.wait_ge(wv_ready, t - TPB + 1)
                        nc.scalar.activation(v_sb[:, i, :], v_win[:, 0:WIN * D], ACT.Copy).then_inc(v_copied, 1)
                        if i == 0:
                            act.wait_ge(x_loaded, 16 * (b + 1))
                        if not first_tile(b, i):
                            act.wait_ge(x_squared, t)
                        if not is_first(b):
                            act.wait_ge(w_ready, 2 * b + i // 2 - 1)
                        nc.scalar.activation(x_sq[:, :], x_sb[:, t, :], ACT.Square, scale=SQ_SCALE,
                                             accum_out=x_ss[:, i:i + 1]).then_inc(x_squared, 1)
                        if not is_first(b):
                            copy_out(t - LAG, i)

                over_batches(act, body)
                for t in range(NT - LAG, NT):
                    attention_high(t, t)
                    copy_out(t, t)

            either(act, run)

        @block.vector
        def _(dve):
            dve.wait_ge(idx_here, 16)
            nc.vector.tensor_reduce(idx_max[:, :], idx_sb[:, :], AX.X, ALU.max)
            nc.vector.tensor_reduce(idx_min[:, :], idx_sb[:, :], AX.X, ALU.min).then_inc(outside_step, 1)
            dve.wait_ge(outside_step, 1)
            nc.vector.tensor_scalar(above[:, :], idx_max[:, :], float(BLK - 1), None, ALU.is_gt).then_inc(outside_step, 1)
            dve.wait_ge(outside_step, 2)
            nc.vector.scalar_tensor_tensor(outside[:, :], idx_min[:, :], 0.0, above[:, :], ALU.is_lt,
                                           ALU.max).then_inc(outside_step, 1)
            dve.wait_ge(row_step, 1)
            nc.vector.tensor_scalar(row_and[:, :], row_i32[:, :], BLK - 1, None, ALU.bitwise_and).then_inc(row_step, 1)
            dve.wait_ge(row_step, 2)
            nc.vector.tensor_copy(row_of[:, :], row_and[:, :]).then_inc(row_step, 1)
            dve.wait_ge(outside_summed, 1)
            nc.vector.tensor_copy(path_flag[0:1, 0:1], q_ps[0:1, 0:1]).then_inc(flag_ready, 1)
            dve.wait_ge(row_step, 3)

            def ctx_norms(g, slots, n):
                dve.wait_ge(ctx_squared, n)
                if not is_first(g):
                    dve.wait_ge(ctx_rms, g)
                nc.vector.tensor_scalar(c_var[:, slots], c_ss[:, slots], 1.0 / D, EPS_RMS, ALU.mult, ALU.add).then_inc(ctx_var, 1)
                dve.wait_ge(ctx_root, g + 1)
                nc.vector.reciprocal(c_r0[:, slots], c_root[:, slots]).then_inc(rms_step, 1)
                dve.wait_ge(rms_step, 4 * g + 1)
                nc.vector.tensor_tensor(c_r0sq[:, slots], c_r0[:, slots], c_r0[:, slots], ALU.mult).then_inc(rms_step, 1)
                dve.wait_ge(rms_step, 4 * g + 2)
                nc.vector.tensor_tensor(c_vr[:, slots], c_r0sq[:, slots], c_var[:, slots], ALU.mult).then_inc(rms_step, 1)
                dve.wait_ge(rms_step, 4 * g + 3)
                nc.vector.tensor_scalar(c_fix[:, slots], c_vr[:, slots], -0.5, 1.5, ALU.mult, ALU.add).then_inc(rms_step, 1)
                dve.wait_ge(rms_step, 4 * g + 4)
                nc.vector.tensor_tensor(c_rms[:, slots], c_r0[:, slots], c_fix[:, slots], ALU.mult).then_inc(ctx_rms, 1)

            def ctx_low(u, slot):
                dve.wait_ge(cT_high, u + 1)
                nc.vector.tensor_tensor(cT_hl[:, 1, :, :].rearrange("p k r -> p (k r)"), cT[:, slot, :],
                                        cT_hl[:, 0, :, :].rearrange("p k r -> p (k r)").bitcast(F32),
                                        ALU.subtract).then_inc(cT_split, 1)

            def kv_low(u, slot):
                dve.wait_ge(hi_ready, u + 1)
                nc.vector.scalar_tensor_tensor(kv_lo[:, :], kv_ps[0:ROWS, :], c_rms[:, :].unsqueeze(2)[:, slot, :],
                                               kv_hi[:, :].bitcast(F32), ALU.mult, ALU.subtract).then_inc(lo_ready, 1)

            idx_tiles = idx_bc[:, :, :].rearrange("p b (i t) -> p (b i) t", t=P)

            def make_onehot(path, t, i):
                for c, blk in enumerate(path.blocks):
                    last = nc.vector.tensor_scalar(onehot[:, i if path.ahead else c, :], idx_tiles[:, t, :],
                                                   float(BLK * blk), row_of[:, :], ALU.subtract, ALU.is_equal)
                last.then_inc(onehot_ready, 1)

            def attention_low(t, i):
                dve.wait_ge(aT_high, t + 1)
                nc.vector.tensor_tensor(aT_hl[:, i % 2, 1, :, :].rearrange("p k t -> p (k t)"), a_ps[:, 0:D],
                                        aT_hl[:, i % 2, 0, :, :].rearrange("p k t -> p (k t)").bitcast(F32),
                                        ALU.subtract).then_inc(aT_split, 1)

            def weights(b, i):
                pair = 2 * b + i // 2 - 1
                t = TPB * b + i
                at = (i - 2) % TPB
                both = slice(at, at + 2)

                def square():
                    dve.wait_ge(score_ready, t)
                    nc.vector.scalar_tensor_tensor(w_raw[:, :, :], score[:, both, :], 0.0, score[:, both, :],
                                                   ALU.max, ALU.mult).then_inc(squared_ready, 1)

                def sums():
                    dve.wait_ge(squared_ready, pair + 1)
                    nc.vector.tensor_reduce(den[:, :, :], w_raw[:, :, :].rearrange("p t (j h) -> p t h j", j=WIN),
                                            AX.X, ALU.add).then_inc(den_step, 1)

                def bound():
                    dve.wait_ge(den_step, 3 * pair + 1)
                    dve.wait_ge(x_squared, t)
                    nc.vector.scalar_tensor_tensor(den_max[:, :, :], x_ss[:, both].unsqueeze(2).to_broadcast([P, 2, H]),
                                                   DEN_LEAST, den[:, :, :], ALU.add, ALU.max).then_inc(den_step, 1)

                def invert():
                    dve.wait_ge(den_step, 3 * pair + 2)
                    nc.vector.reciprocal(den_inv[:, :, :], den_max[:, :, :]).then_inc(den_step, 1)

                def normalize():
                    dve.wait_ge(den_step, 3 * pair + 3)
                    if not (isinstance(pair, int) and pair < 2):
                        dve.wait_ge(wv_ready, t - TPB)
                    nc.vector.tensor_tensor(
                        w_sb[:, both, :].rearrange("p t (j h) -> p t j h", j=WIN),
                        w_raw[:, :, :].rearrange("p t (j h) -> p t j h", j=WIN),
                        den_inv[:, :, :].unsqueeze(2).to_broadcast([P, 2, WIN, H]), ALU.mult).then_inc(w_ready, 1)

                return square, sums, bound, invert, normalize

            def run(path):
                dve.wait_ge(wkv_high, 1)
                for k in range(KC):
                    last = nc.vector.scalar_tensor_tensor(wkv_hl[:, 1, k, :], wkv_raw[:, k, :], gkv_sb[:, k:k + 1],
                                                          wkv_hl[:, 0, k, :].bitcast(F32), ALU.mult, ALU.subtract)
                last.then_inc(wkv_split, 1)
                if path.ahead:
                    ctx_low(0, 0)
                    ctx_norms(0, slice(0, 1), 1)
                dve.wait_ge(wq_high, 1)
                for k in range(KC):
                    last = nc.vector.scalar_tensor_tensor(wq_hl[:, 1, k, :], wq_raw[:, k, :], gq_sb[:, k:k + 1],
                                                          wq_hl[:, 0, k, :].bitcast(F32), ALU.mult, ALU.subtract)
                last.then_inc(wq_split, 1)
                if path.ahead:
                    kv_low(0, 0)
                    dve.wait_ge(idx_loaded, 16)
                    make_onehot(path, 0, 0)
                    make_onehot(path, 1, 1)
                    ctx_norms(1, slice(1, B), B)

                def body(b):
                    if not path.ahead:
                        ctx_norms(b, slice(0, NBLK), NBLK * (b + 1))
                        for u, slot in path.units(b):
                            ctx_low(u, slot)
                            kv_low(u, slot)
                        dve.wait_ge(idx_loaded, 16 * (b + 1))
                    for i in range(TPB):
                        t = TPB * b + i
                        steps = [lambda: None] * 5
                        if i % 2 == 0 and (not is_first(b) or i > 0):
                            steps = weights(b, i)
                        steps[0]()
                        if path.ahead and not is_last(b) and i == 0:
                            ctx_low(b + 1, b + 1)
                        if not is_first(b):
                            attention_low(t - LAG, i)
                        steps[1]()
                        if not path.ahead:
                            if not first_tile(b, i):
                                dve.wait_ge(v_ready, t)
                            make_onehot(path, t, i)
                        elif not (is_last(b) and i >= 2):
                            if i == 2:
                                dve.wait_ge(idx_loaded, 16 * (b + 2))
                            if not is_first(b) or i >= 2:
                                dve.wait_ge(v_ready, t - 1)
                            make_onehot(path, t + 2, (i + 2) % TPB)
                        steps[2]()
                        if path.ahead and not is_last(b) and i == 1:
                            kv_low(b + 1, b + 1)
                        dve.wait_ge(q_copied, t + 1)
                        dve.wait_ge(k_ready, t + 1)
                        nc.vector.tensor_tensor(
                            prod[:, i % 2, :].rearrange("p (j d) -> p j d", j=WIN),
                            k_win[:, 0:WIN * D].rearrange("p (j d) -> p j d", j=WIN),
                            q_sb[:, i % 2, :].unsqueeze(1).to_broadcast([P, WIN, D]), ALU.mult).then_inc(prod_ready, 1)
                        steps[3]()
                        dve.wait_ge(prod_ready, t + 1)
                        nc.vector.tensor_reduce(score[:, i, :], prod[:, i % 2, :].rearrange("p (a d) -> p a d", d=HD),
                                                AX.X, ALU.add).then_inc(score_ready, 1)
                        steps[4]()

                over_batches(dve, body)
                for step in weights(B, 0):
                    step()
                for t in range(NT - LAG, NT):
                    attention_low(t, t)

            either(dve, run)

        @block.tensor
        def _(pe):
            pe.wait_ge(outside_step, 3)
            pe.wait_ge(ones_ready, 1)
            nc.tensor.matmul(q_ps[0:1, 0:1], outside[:, :], ones[:, 0:1], start=True, stop=True).then_inc(outside_summed, 1)

            def project(to, columns, weights_hl):
                for n, (x, y) in enumerate(PARTS):
                    for k in range(KC):
                        last = nc.tensor.matmul(to, columns[:, x, k, :], weights_hl[:, y, k, :],
                                                start=(n == 0 and k == 0), stop=(n == len(PARTS) - 1 and k == KC - 1))
                return last

            def kv_project(u):
                pe.wait_ge(cT_split, u + 1)
                if not is_first(u):
                    pe.wait_ge(lo_ready, u)
                project(kv_ps[0:ROWS, :], cT_hl, wkv_hl).then_inc(kv_ready, 1)

            def gather(path, b, i, to, at, done):
                n = len(path.blocks)
                for j in range(WIN):
                    for c in range(n):
                        last = nc.tensor.matmul(to[:, j * D:(j + 1) * D], onehot[:, i if path.ahead else c, :],
                                                table[:, b if path.ahead else c, j, at:at + D],
                                                start=(c == 0), stop=(c == n - 1))
                last.then_inc(done, 1)

            def transpose_sum(t, i):
                pe.wait_ge(wv_ready, t + 1)
                if not is_first(t):
                    pe.wait_ge(aT_split, t)
                for k in range(KC):
                    for j in range(WIN):
                        last = nc.tensor.matmul(a_ps[:, k * P:(k + 1) * P], wv[:, i % 2, j * D + k * P:j * D + (k + 1) * P],
                                                ident[:, :], start=(j == 0), stop=(j == WIN - 1), is_transpose=True)
                last.then_inc(aT_ready, 1)

            def project_out(t, i):
                pe.wait_ge(aT_split, t + 1)
                if not is_first(t):
                    pe.wait_ge(o_copied, t)
                project(o_ps[:, 0:D], aT_hl[:, i % 2], wo_hl).then_inc(o_ready, 1)

            def run(path):
                pe.wait_ge(wkv_split, 1)
                if path.ahead:
                    kv_project(0)
                pe.wait_ge(wq_split, 1)

                def body(b):
                    if not path.ahead:
                        for u, _ in path.units(b):
                            kv_project(u)
                    for i in range(TPB):
                        t = TPB * b + i
                        if not is_first(b):
                            transpose_sum(t - LAG, i)
                        pe.wait_ge(xT_split, t + 1)
                        if not first_tile(b, i):
                            pe.wait_ge(q_copied, t)
                        project(q_ps[:, 0:D], xT_hl[:, i], wq_hl).then_inc(q_ready, 1)
                        if i == 0:
                            pe.wait_ge(table_loaded, 32 * WIN * len(path.blocks) * (b + 1))
                        pe.wait_ge(onehot_ready, t + 1)
                        if not first_tile(b, i):
                            pe.wait_ge(prod_ready, t)
                        gather(path, b, i, k_win, 0, k_ready)
                        if not first_tile(b, i):
                            pe.wait_ge(v_copied, t)
                        gather(path, b, i, v_win, D, v_ready)
                        if path.ahead and not is_last(b) and i == 0:
                            kv_project(b + 1)
                        if not is_first(b):
                            project_out(t - LAG, i)
                    if is_first(b):
                        pe.wait_ge(wo_split, 1)

                pe.wait_ge(ident_ready, 1)
                over_batches(pe, body)
                for t in range(NT - LAG, NT):
                    transpose_sum(t, t)
                    project_out(t, t)

            either(pe, run)


def kernel(x, ctx_1024, itok_BxS_0_255, L0_xattn_gamma_q, L0_xattn_gamma_kv, L0_xattn_Wq, L0_xattn_Wk, L0_xattn_Wv,
           L0_xattn_Wo):
    import numpy as np
    import concourse.bacc as bacc
    from concourse.bass_utils import run_bass_kernel_spmd

    x, ctx, idx = np.asarray(x), np.asarray(ctx_1024), np.asarray(itok_BxS_0_255)
    wq, wk, wv, wo = (np.asarray(w) for w in (L0_xattn_Wq, L0_xattn_Wk, L0_xattn_Wv, L0_xattn_Wo))
    gq, gkv = np.asarray(L0_xattn_gamma_q), np.asarray(L0_xattn_gamma_kv)

    def chunked(a):
        return np.ascontiguousarray(a.reshape(KC, P, -1).transpose(1, 0, 2))

    x_rows = x.reshape(B, P, TPB, D)
    x_cols = x_rows.reshape(B, P, TPB, KC, P).transpose(0, 2, 4, 3, 1)
    idx_cols = idx.reshape(B, P, TPB).transpose(0, 2, 1).reshape(B, S)
    pad = np.zeros((B, BLK + 1, D), ctx.dtype)
    padded = np.concatenate([pad, ctx, pad], axis=1)
    blocks = np.stack([padded[:, c * BLK:c * BLK + ROWS] for c in range(NBLK)], axis=1)
    ctx_cols = blocks.reshape(B, NBLK, ROWS, KC, P).transpose(0, 1, 4, 3, 2)

    arrays = {
        "x_rows": x_rows, "x_cols": x_cols, "ctx_rows": blocks, "ctx_cols": ctx_cols, "idx_cols": idx_cols,
        "idx_all": idx.reshape(P, NT), "gamma_q": gq.reshape(KC, P).T, "gamma_kv": gkv.reshape(KC, P).T,
        "wq": chunked(wq.T), "wkv": chunked(np.concatenate([wk.T, wv.T], axis=1)), "wo": chunked(wo.T),
    }
    arrays = {n: np.ascontiguousarray(a) for n, a in arrays.items()}
    nc = bacc.Bacc("TRN2", target_bir_lowering=False, num_devices=1)
    aps = {n: nc.dram_tensor(n, a.shape, mybir.dt.from_np(a.dtype), kind="ExternalInput").ap() for n, a in arrays.items()}
    out = nc.dram_tensor("out", (B, P, TPB, D), F32, kind="ExternalOutput").ap()
    window_attention(nc, **aps, out=out)
    r = run_bass_kernel_spmd(nc, [arrays], core_ids=[0])
    return r.results[0]["out"].reshape(B, S, D)
```

```python
from contextlib import ExitStack

import concourse.bass as bass
from concourse import mybir

F32 = mybir.dt.float32
F32R = mybir.dt.float32r
I32 = mybir.dt.int32
ALU = mybir.AluOpType
ACT = mybir.ActivationFunctionType
AX = mybir.AxisListType

B, S, D, H = 8, 512, 256, 16
HD = D // H
P = 128
KC = D // P
TPB = S // P
NT = B * TPB
WIN = 3
BLK = 64
ROWS = BLK + WIN - 1
NBLK = S // BLK + 2
EPS_RMS = 1.1920929e-07
EPS_DEN = 1e-06
SQ_SCALE = (HD * EPS_DEN / D) ** 0.5
DEN_LEAST = HD * EPS_DEN * EPS_RMS
AHEAD = 2
LAG = TPB
WARM = 4
PARTS = ((0, 0), (1, 0), (0, 1))


class Path:

    def __init__(self, blocks, ahead):
        self.blocks = blocks
        self.ahead = ahead

    def units(self, b):
        if self.ahead:
            return [(b, b)]
        return [(b * len(self.blocks) + c, c) for c in range(len(self.blocks))]

    def moved(self, u):
        return u - 1 if self.ahead else u


NEAR = Path([0], True)
ANY = Path(list(range(-1, NBLK - 1)), False)


def is_first(n):
    return isinstance(n, int) and n == 0


def is_last(b):
    return isinstance(b, int) and b == B - 1


def first_part(b):
    return 1 if is_first(b) else 0


def makes_table(path, b):
    return path.ahead and not (isinstance(b, int) and b + AHEAD >= B)


def first_tile(b, i):
    return is_first(b) and i == 0


def wait_all(eng, *waits):
    for _, n in waits:
        if not isinstance(n, int):
            eng.compute_val(n)
    for sem, n in waits:
        eng.wait_ge(sem, n)


def over_batches(eng, body, alone=1):
    for b in range(alone):
        body(b)
    with eng.Fori(alone, B - AHEAD) as b:
        body(b)
    for b in range(B - AHEAD, B):
        body(b)


def window_attention(nc, x_rows, x_cols, ctx_rows, ctx_cols, idx_cols, idx_all, gammas, wq, wkv, wo, out):
    with ExitStack() as stack:
        def sb(name, shape, dt=F32):
            return stack.enter_context(nc.sbuf_tensor(name, shape, dt))

        def pb(name, shape):
            return stack.enter_context(nc.psum_tensor(name, shape, F32))

        def sem(name):
            return stack.enter_context(nc.semaphore(name))

        wo_raw = sb("wo_raw", [P, KC, D])
        wq_hl = sb("wq_hl", [P, 2, KC, D], F32R)
        wkv_hl = sb("wkv_hl", [P, 2, KC, 2 * D], F32R)
        wo_hl = sb("wo_hl", [P, 2, KC, D], F32R)
        gamma_sb = sb("gamma_sb", [P, 2, KC])
        gq_sb = gamma_sb[:, 0, :]
        gkv_sb = gamma_sb[:, 1, :]
        ident = sb("ident", [P, P])
        ones = sb("ones", [P, P])
        idx_sb = sb("idx_sb", [P, NT], I32)
        idx_max = sb("idx_max", [P, 1])
        idx_min = sb("idx_min", [P, 1])
        above = sb("above", [P, 1])
        outside = sb("outside", [P, 1])
        path_flag = sb("path_flag", [1, 1], I32)
        x_sb = sb("x_sb", [P, NT, D])
        xT = sb("xT", [P, TPB, KC, P])
        xT_hl = sb("xT_hl", [P, TPB, 2, KC, P], F32R)
        idx_bc = sb("idx_bc", [P, B, S], I32)
        row_i32 = sb("row_i32", [P, 1], I32)
        row_and = sb("row_and", [P, 1], I32)
        row_of = sb("row_of", [P, 1])
        minus_row = sb("minus_row", [P, 1])
        far = sb("far", [P, 2 * P])
        onehot = sb("onehot", [P, NBLK, P], F32R)
        cT = sb("cT", [P, NBLK, KC * ROWS])
        cT_hl = sb("cT_hl", [P, 2, KC, ROWS], F32R)
        c_rows = sb("c_rows", [P, NBLK, D])
        c_sq = sb("c_sq", [ROWS, D])
        c_ss = sb("c_ss", [ROWS, NBLK])
        c_var = sb("c_var", [ROWS, NBLK])
        c_root = sb("c_root", [ROWS, NBLK])
        c_r0 = sb("c_r0", [ROWS, NBLK])
        c_r0sq = sb("c_r0sq", [ROWS, NBLK])
        c_vr = sb("c_vr", [ROWS, NBLK])
        c_fix = sb("c_fix", [ROWS, NBLK])
        c_rms = sb("c_rms", [ROWS, NBLK])
        shift = sb("shift", [P, WIN, P])
        first_rms = sb("first_rms", [P, WIN])
        kv_hi = sb("kv_hi", [ROWS, 2 * D], F32R)
        kv_lo = sb("kv_lo", [ROWS, 2 * D], F32R)
        table = sb("table", [P, max(B, NBLK), WIN, 2 * D], F32R)
        x_sq = sb("x_sq", [P, D])
        x_ss = sb("x_ss", [P, TPB])
        q_sb = sb("q_sb", [P, 2, D])
        prod = sb("prod", [P, 2, WIN * D])
        score = sb("score", [P, TPB, WIN * H])
        w_raw = sb("w_raw", [P, 2, WIN * H])
        den = sb("den", [P, 2, H])
        den_max = sb("den_max", [P, 2, H])
        den_inv = sb("den_inv", [P, 2, H])
        w_sb = sb("w_sb", [P, TPB, WIN * H])
        v_sb = sb("v_sb", [P, TPB, WIN * D])
        wq_raw = v_sb[:, TPB - 1, 0:KC * D].rearrange("p (k n) -> p k n", k=KC)
        first_hl = table[:, B, :, :].rearrange("p j n -> p (j n)").rearrange("p (x j k m) -> p x j k m", x=2, j=WIN, k=KC)
        first_cT = cT[:, 0, :].rearrange("p (k r) -> p k r", k=KC)
        cT_sq = c_rows[:, :, :].rearrange("p u d -> p (u d)")[:, 0:B * KC * ROWS].rearrange(
            "p (u k r) -> p u k r", u=B, k=KC)
        wv = sb("wv", [P, 2, WIN * D])
        aT_hl = sb("aT_hl", [P, 2, 2, KC, P], F32R)
        o_sb = sb("o_sb", [P, TPB, D])
        wkv_raw = o_sb[:, :, :].rearrange("p t d -> p (t d)").rearrange("p (k n) -> p k n", k=KC)

        k_ps = pb("k_ps", [P, 2, 512])
        v_ps = pb("v_ps", [P, 2, 512])
        q_ps = pb("q_ps", [P, 512])
        a_ps = pb("a_ps", [P, 512])
        o_ps = pb("o_ps", [P, 512])
        kv_ps = pb("kv_ps", [P, 512])
        k_win = k_ps[:, :, :].rearrange("p a b -> p (a b)")
        v_win = v_ps[:, :, :].rearrange("p a b -> p (a b)")

        idx_here = sem("idx_here")
        wkv_here = sem("wkv_here")
        wq_here = sem("wq_here")
        wo_here = sem("wo_here")
        wkv_high = sem("wkv_high")
        wkv_split = sem("wkv_split")
        wq_high = sem("wq_high")
        wq_split = sem("wq_split")
        wo_high = sem("wo_high")
        wo_split = sem("wo_split")
        ones_ready = sem("ones_ready")
        ident_ready = sem("ident_ready")
        outside_step = sem("outside_step")
        outside_summed = sem("outside_summed")
        flag_ready = sem("flag_ready")
        row_step = sem("row_step")
        xT_loaded = [sem(f"xT_loaded{i}") for i in range(0, TPB, 2)]
        xT_high = sem("xT_high")
        xT_split = sem("xT_split")
        x_loaded = sem("x_loaded")
        idx_loaded = sem("idx_loaded")
        ctx_first = sem("ctx_first")
        ctx_loaded = sem("ctx_loaded")
        ctx_squared = sem("ctx_squared")
        ctx_var = sem("ctx_var")
        ctx_root = sem("ctx_root")
        rms_step = sem("rms_step")
        ctx_rms = sem("ctx_rms")
        cT_high = sem("cT_high")
        cT_split = sem("cT_split")
        kv_ready = sem("kv_ready")
        cT_squared = sem("cT_squared")
        squares_summed = sem("squares_summed")
        shift_ready = sem("shift_ready")
        shifted = sem("shifted")
        first_rms_ready = sem("first_rms_ready")
        first_cT_high = sem("first_cT_high")
        first_cT_split = sem("first_cT_split")
        first_ready = sem("first_ready")
        first_high = sem("first_high")
        hi_ready = sem("hi_ready")
        lo_ready = sem("lo_ready")
        table_loaded = sem("table_loaded")
        onehot_ready = sem("onehot_ready")
        far_ready = sem("far_ready")
        x_squared = sem("x_squared")
        q_ready = sem("q_ready")
        q_copied = sem("q_copied")
        k_ready = sem("k_ready")
        v_ready = sem("v_ready")
        v_copied = sem("v_copied")
        prod_ready = sem("prod_ready")
        score_ready = sem("score_ready")
        squared_ready = sem("squared_ready")
        den_step = sem("den_step")
        w_ready = sem("w_ready")
        wv_ready = sem("wv_ready")
        wv_here = sem("wv_here")
        aT_ready = sem("aT_ready")
        aT_high = sem("aT_high")
        aT_split = sem("aT_split")
        o_ready = sem("o_ready")
        o_copied = sem("o_copied")
        res_ready = sem("res_ready")
        end_ready = sem("end_ready")
        stored = sem("stored")

        idx_pairs = idx_bc[:, :, :].rearrange("p b (i t) -> p (b i) t", t=2 * P)
        idx_tiles = idx_bc[:, :, :].rearrange("p b (i t) -> p (b i) t", t=P)

        def weigh(engine, i):
            return engine.tensor_tensor(
                wv[:, i % 2, :].rearrange("p (a d) -> p a d", d=HD), v_sb[:, i, :].rearrange("p (a d) -> p a d", d=HD),
                w_sb[:, i, :].unsqueeze(2).to_broadcast([P, WIN * H, HD]), ALU.mult)

        first_banks = (a_ps, o_ps, kv_ps)

        def a_bank(t):
            return (a_ps, q_ps)[t % 2]

        def o_bank(t):
            return (o_ps, kv_ps)[t % 2]

        block = stack.enter_context(nc.Block())

        def either(eng, run):
            eng.wait_ge(flag_ready, 1)
            flag = eng.value_load(path_flag[0:1, 0:1], min_val=0, max_val=P)
            with eng.If(flag == 0):
                run(NEAR)
            with eng.Else():
                run(ANY)

        @block.sync
        def _(sp):
            def load_columns(b, i):
                sp.dma_start(xT[:, i:i + 2, :, :], x_cols[b, i // 2]).then_inc(xT_loaded[i // 2], 16)

            def load_tokens(b):
                if not is_first(b):
                    sp.wait_ge(x_loaded, b * 16)
                    sp.wait_ge(idx_loaded, b * 16)
                sp.dma_start(idx_bc[:, b, :], idx_cols[b].partition_broadcast(P)).then_inc(idx_loaded, 16)
                sp.dma_start(x_sb[:, :, :].rearrange("p (b i) d -> p b i d", i=TPB)[:, b, :, :],
                             x_rows[b]).then_inc(x_loaded, 16)

            sp.dma_start(idx_sb[:, :], idx_all).then_inc(idx_here, 16)
            sp.dma_start(cT[:, 0:AHEAD, :],
                         ctx_cols[0:AHEAD, 1].rearrange("b p k r -> p b (k r)")).then_inc(ctx_first, 16)
            sp.dma_start(gamma_sb[:, :, :], gammas).then_inc(wkv_here, 16)
            sp.dma_start(wkv_raw[:, :, :], wkv).then_inc(wkv_here, 16)
            load_columns(0, 0)
            sp.dma_start(wq_raw[:, :, :], wq).then_inc(wq_here, 16)
            load_tokens(0)
            load_columns(0, 2)
            sp.dma_start(cT[:, AHEAD:B, :],
                         ctx_cols[AHEAD:B, 1].rearrange("b p k r -> p b (k r)")).then_inc(ctx_loaded, 16)
            sp.dma_start(wo_raw[:, :, :], wo).then_inc(wo_here, 16)

            def load_context(b):
                if not is_first(b):
                    sp.wait_ge(cT_split, b * NBLK)
                sp.wait_ge(ctx_loaded, b * 32 + 16)
                if is_first(b):
                    sp.wait_ge(ctx_first, 16)
                if not is_first(b):
                    sp.wait_ge(ctx_squared, b * NBLK)
                sp.dma_start(c_rows[0:ROWS, :, :], ctx_rows[b].rearrange("c r d -> r c d")).then_inc(ctx_loaded, 16)
                sp.dma_start(cT[:, :, :], ctx_cols[b].rearrange("c p k r -> p c (k r)")).then_inc(ctx_loaded, 16)

            def place_table(u, slot, tiles=None):
                if tiles is None:
                    sp.wait_ge(hi_ready, u + 1)
                else:
                    wait_all(sp, (v_ready, tiles), (hi_ready, u + 1))
                dst = table[:, slot, :, :]
                for j in range(WIN):
                    sp.dma_start(dst[0:BLK, j, :].bitcast(F32), kv_hi[j:j + BLK, :].bitcast(F32)).then_inc(table_loaded, 16)
                sp.wait_ge(lo_ready, u + 1)
                for j in range(WIN):
                    sp.dma_start(dst[BLK:P, j, :].bitcast(F32), kv_lo[j:j + BLK, :].bitcast(F32)).then_inc(table_loaded, 16)

            def store(b, i):
                if is_last(b):
                    sp.wait_ge(end_ready, i + 2)
                else:
                    sp.wait_ge(res_ready, TPB * b + i + 2)
                rows = x_sb[:, :, :].rearrange("p (b i) d -> p b i d", i=TPB)
                sp.dma_start(out[b][:, i:i + 2, :], rows[:, b, i:i + 2, :]).then_inc(stored, 16)

            def run(path):
                def body(b):
                    if not path.ahead:
                        load_context(b)
                        for u, slot in path.units(b):
                            place_table(u, slot, TPB * b if slot == 0 and not is_first(b) else None)
                    if path.ahead and not (is_first(b) or is_last(b)):
                        place_table(b + 1, b + 1)
                    for i in range(0, TPB, 2):
                        if not is_last(b):
                            sp.wait_ge(xT_split, TPB * b + i + 2)
                            load_columns(b + 1, i)
                        if i == 0 and not is_last(b):
                            load_tokens(b + 1)
                        if path.ahead and first_tile(b, i):
                            place_table(1, 1)
                    if not (isinstance(b, int) and b < 2):
                        store(b - 2, 0)
                        store(b - 2, 2)

                over_batches(sp, body, alone=2)
                for b in range(B - 2, B):
                    store(b, 0)
                    store(b, 2)
                sp.wait_ge(stored, 16 * 2 * B)

            either(sp, run)

        @block.gpsimd
        def _(pool):
            nc.gpsimd.memset(ones[:, :], 1.0).then_inc(ones_ready, 1)
            nc.gpsimd.iota(row_i32[:, :], pattern=[[0, 1]], base=0, channel_multiplier=1).then_inc(row_step, 1)
            pool.wait_ge(ones_ready, 1)
            nc.gpsimd.affine_select(out=ident[:, :], in_=ones[:, :], compare_op=ALU.is_equal, fill=0.0, base=0,
                                    pattern=[[-1, P]], channel_multiplier=1).then_inc(ident_ready, 1)
            for j in range(WIN):
                last = nc.gpsimd.affine_select(out=shift[:, j, :].rearrange("p (h r) -> p h r", h=2),
                                               in_=ones[:, :].rearrange("p (h r) -> p h r", h=2),
                                               compare_op=ALU.is_equal, fill=0.0, base=-j,
                                               pattern=[[0, 2], [-1, BLK]], channel_multiplier=1)
            last.then_inc(shift_ready, 1)

            def split_columns(t, i):
                pool.wait_ge(xT_high, t + 1)
                nc.gpsimd.tensor_tensor(xT_hl[:, i, 1, :, :], xT[:, i, :, :], xT_hl[:, i, 0, :, :].bitcast(F32),
                                        ALU.subtract).then_inc(xT_split, 1)

            def residual(t, i):
                pool.wait_ge(o_copied, t + 1)
                nc.gpsimd.tensor_tensor(x_sb[:, t, :], o_sb[:, i % TPB, :], x_sb[:, t, :], ALU.add).then_inc(res_ready, 1)

            def square_columns(first, end, loaded):
                pool.wait_ge(loaded, 16)
                nc.gpsimd.tensor_tensor(cT_sq[:, first:end, :, :].rearrange("p u k r -> p (u k r)"),
                                        cT[:, first:end, :].rearrange("p u n -> p (u n)"),
                                        cT[:, first:end, :].rearrange("p u n -> p (u n)"), ALU.mult).then_inc(cT_squared, 1)

            def run(path):
                if path.ahead:
                    square_columns(0, AHEAD, ctx_first)
                split_columns(0, 0)
                split_columns(1, 1)
                if path.ahead:
                    square_columns(AHEAD, B, ctx_loaded)
                pool.wait_ge(wo_here, 16)
                nc.gpsimd.tensor_copy(wo_hl[:, 0, :, :], wo_raw[:, :, :]).then_inc(wo_high, 1)
                pool.wait_ge(wo_high, 1)
                nc.gpsimd.tensor_tensor(wo_hl[:, 1, :, :], wo_raw[:, :, :], wo_hl[:, 0, :, :].bitcast(F32),
                                        ALU.subtract).then_inc(wo_split, 1)
                for i in range(2, TPB):
                    split_columns(i, i)

                def body(b):
                    for i in range(TPB):
                        t = TPB * b + i
                        if not is_last(b):
                            split_columns(t + TPB, i)
                        if is_last(b) and i == 2:
                            continue
                        pool.wait_ge(w_ready, 2 * b + i // 2 + 1)
                        pool.wait_ge(v_copied, t + 1)
                        if not is_first(b) or i >= 2:
                            pool.wait_ge(aT_ready, t - 1)
                        weigh(nc.gpsimd, i).then_inc(wv_ready, 1)
                        if is_last(b) and i == 3:
                            residual(NT - LAG - 1, 3)
                        elif not is_first(b) or i == 3:
                            residual(t - 3, (i + 1) % TPB)

                over_batches(pool, body)

            either(pool, run)

        @block.scalar
        def _(act):
            act.wait_ge(ones_ready, 1)
            nc.scalar.activation(c_root[0:1, 0:1], ones[0:1, 0:1], ACT.Sqrt)

            def ctx_square(u, slot, loads):
                act.wait_ge(ctx_loaded, loads)
                if not is_first(u):
                    act.wait_ge(ctx_squared, u)
                nc.scalar.activation(c_sq[:, :], c_rows[0:ROWS, slot, :], ACT.Square,
                                     accum_out=c_ss[:, :].unsqueeze(2)[:, slot, :]).then_inc(ctx_squared, 1)

            def ctx_sqrt(g, slots):
                act.wait_ge(ctx_var, g + 1)
                nc.scalar.activation(c_root[:, slots], c_var[:, slots], ACT.Sqrt).then_inc(ctx_root, 1)

            def ctx_high(path, u, slot):
                if path.ahead and is_first(u - AHEAD):
                    act.wait_ge(ctx_loaded, 16)
                if not is_first(path.moved(u)):
                    act.wait_ge(kv_ready, u)
                nc.scalar.activation(cT_hl[:, 0, :, :].rearrange("p k r -> p (k r)"), cT[:, slot, :],
                                     ACT.Copy).then_inc(cT_high, 1)

            def kv_high(path, g, u, slot):
                act.wait_ge(kv_ready, u + 1)
                act.wait_ge(ctx_rms, g + 1)
                if not is_first(path.moved(u)):
                    act.wait_ge(table_loaded, path.moved(u) * 32 * WIN)
                nc.scalar.activation(kv_hi[:, :], kv_ps[0:ROWS, :], ACT.Copy,
                                     scale=c_rms[:, :].unsqueeze(2)[:, slot, :]).then_inc(hi_ready, 1)

            def first_columns_high(j):
                act.wait_ge(ctx_first, 16)
                nc.scalar.activation(first_hl[:, 0, j, :, :].rearrange("p k (h r) -> p k h r", h=2),
                                     first_cT[:, :, j:j + BLK].unsqueeze(2).to_broadcast([P, KC, 2, BLK]),
                                     ACT.Copy).then_inc(first_cT_high, 1)

            def first_table_high(j):
                act.wait_ge(*((kv_ready, 1) if j == WIN - 1 else (first_ready, j + 1)))
                act.wait_ge(first_rms_ready, 1)
                nc.scalar.activation(table[:, 0, j, :], first_banks[j][:, :], ACT.Copy,
                                     scale=first_rms[:, j:j + 1]).then_inc(
                    hi_ready if j == WIN - 1 else first_high, 1)

            def columns_high(t, i, loads):
                act.wait_ge(xT_loaded[i // 2], loads)
                nc.scalar.activation(xT_hl[:, i, 0, :, :], xT[:, i, :, :], ACT.Copy).then_inc(xT_high, 1)

            def index_distance(pair):
                if not is_first(pair):
                    act.wait_ge(onehot_ready, 2 * pair)
                nc.scalar.activation(far[:, :], idx_pairs[:, pair, :], ACT.Abs, bias=minus_row[:, :]).then_inc(far_ready, 1)

            def make_onehot(i):
                nc.scalar.activation(onehot[:, i:i + 2, :].rearrange("p i t -> p (i t)"), far[:, :], ACT.Relu,
                                     bias=1.0, scale=-1.0).then_inc(onehot_ready, 2)

            def attention_high(t, i, bank=a_ps):
                act.wait_ge(aT_ready, t + 1)
                nc.scalar.activation(aT_hl[:, i % 2, 0, :, :].rearrange("p k t -> p (k t)"), bank[:, 0:D],
                                     ACT.Copy).then_inc(aT_high, 1)

            def copy_out(t, i):
                act.wait_ge(o_ready, t + 1)
                nc.scalar.activation(o_sb[:, i % TPB, :], o_ps[:, 0:D], ACT.Copy).then_inc(o_copied, 1)

            def run(path):
                if path.ahead:
                    for j in range(WIN):
                        first_columns_high(j)
                act.wait_ge(wkv_here, 32)
                for k in range(KC):
                    nc.scalar.activation(wkv_hl[:, 0, k, :], wkv_raw[:, k, :], ACT.Copy,
                                         scale=gkv_sb[:, k:k + 1]).then_inc(wkv_high, 1)
                    if path.ahead and k == 0:
                        ctx_sqrt(0, slice(0, AHEAD))
                columns_high(0, 0, 16)
                columns_high(1, 1, 16)
                if path.ahead:
                    ctx_high(path, 1, 1)
                    first_table_high(0)
                act.wait_ge(wq_here, 16)
                for k in range(KC):
                    last = nc.scalar.activation(wq_hl[:, 0, k, :], wq_raw[:, k, :], ACT.Copy, scale=gq_sb[:, k:k + 1])
                last.then_inc(wq_high, 1)
                if path.ahead:
                    first_table_high(1)
                    act.wait_ge(row_step, 3)
                    act.wait_ge(idx_loaded, 16)
                    index_distance(0)
                    first_table_high(2)
                    act.wait_ge(far_ready, 1)
                    make_onehot(0)

                def square_tokens(b, i):
                    t = TPB * b + i
                    if i == 0:
                        act.wait_ge(x_loaded, 16 * (b + 1))
                    if not first_tile(b, i):
                        act.wait_ge(x_squared, t)
                    if not is_first(b):
                        act.wait_ge(w_ready, 2 * b + i // 2 - 1)
                    nc.scalar.activation(x_sq[:, :], x_sb[:, t, :], ACT.Square, scale=SQ_SCALE,
                                         accum_out=x_ss[:, i:i + 1]).then_inc(x_squared, 1)

                def onehot_pair(b, i):
                    act.wait_ge(far_ready, 2 * b + i // 2 + 2)
                    if not first_tile(b, i):
                        act.wait_ge(v_ready, TPB * b + i)
                    make_onehot((i + 2) % TPB)

                def body(b):
                    if not path.ahead:
                        for u, slot in path.units(b):
                            ctx_square(u, slot, 32 * (b + 1) + 16)
                        ctx_sqrt(b, slice(0, NBLK))
                        for u, slot in path.units(b):
                            ctx_high(path, u, slot)
                            kv_high(path, b, u, slot)
                    for i in range(TPB):
                        t = TPB * b + i
                        if not is_first(b):
                            attention_high(t - LAG, i)
                        if makes_table(path, b) and i == first_part(b):
                            ctx_high(path, b + AHEAD, b + AHEAD)
                        act.wait_ge(q_ready, t + 1)
                        if not is_first(b) or i >= 2:
                            act.wait_ge(prod_ready, t - 1)
                        nc.scalar.activation(q_sb[:, i % 2, :], q_ps[:, 0:D], ACT.Copy).then_inc(q_copied, 1)
                        if i < 2:
                            if not is_first(b):
                                act.wait_ge(q_ready, t - 1)
                            columns_high(t + 2, i + 2, 16 * (b + 1))
                        elif not is_last(b):
                            act.wait_ge(q_ready, t - 1)
                            columns_high(t + 2, i - 2, 16 * (b + 2))
                        if path.ahead and is_first(b) and i == 2:
                            ctx_sqrt(1, slice(AHEAD, B))
                        if path.ahead and is_first(b) and i == 1:
                            kv_high(path, 0, 1, 1)
                        if makes_table(path, b) and not is_first(b) and i == 3:
                            kv_high(path, 1, b + AHEAD, b + AHEAD)
                        if path.ahead and i % 2 == 0 and not (is_last(b) and i == 2):
                            if i == 2:
                                act.wait_ge(idx_loaded, 16 * (b + 2))
                            index_distance(2 * b + i // 2 + 1)
                        if path.ahead and i == 1:
                            onehot_pair(b, 0)
                        act.wait_ge(v_ready, t + 1)
                        if not is_first(b):
                            act.wait_ge(wv_ready, t - TPB + 1)
                        nc.scalar.activation(v_sb[:, i, :], v_win[:, 0:WIN * D], ACT.Copy).then_inc(v_copied, 1)
                        if makes_table(path, b) and is_first(b) and i == 3:
                            kv_high(path, 1, b + AHEAD, b + AHEAD)
                        if path.ahead and i == 2 and not is_last(b):
                            onehot_pair(b, 2)
                        for n in ((0, 1), (2,), (3,), ())[i]:
                            square_tokens(b, n)
                        if not is_first(b):
                            copy_out(t - LAG, i)

                over_batches(act, body)
                for t in range(NT - LAG, NT):
                    attention_high(t, t, a_bank(t))

            either(act, run)

        @block.vector
        def _(dve):
            dve.wait_ge(idx_here, 16)
            nc.vector.tensor_reduce(idx_max[:, :], idx_sb[:, :], AX.X, ALU.max)
            nc.vector.tensor_reduce(idx_min[:, :], idx_sb[:, :], AX.X, ALU.min).then_inc(outside_step, 1)
            dve.wait_ge(outside_step, 1)
            nc.vector.tensor_scalar(above[:, :], idx_max[:, :], float(BLK - 1), None, ALU.is_gt).then_inc(outside_step, 1)
            dve.wait_ge(outside_step, 2)
            nc.vector.scalar_tensor_tensor(outside[:, :], idx_min[:, :], 0.0, above[:, :], ALU.is_lt,
                                           ALU.max).then_inc(outside_step, 1)
            dve.wait_ge(row_step, 1)
            nc.vector.tensor_scalar(row_and[:, :], row_i32[:, :], BLK - 1, None, ALU.bitwise_and).then_inc(row_step, 1)
            dve.wait_ge(row_step, 2)
            nc.vector.tensor_copy(row_of[:, :], row_and[:, :])
            nc.vector.tensor_scalar(minus_row[:, :], row_and[:, :], -1.0, None, ALU.mult).then_inc(row_step, 1)
            dve.wait_ge(outside_summed, 1)
            nc.vector.tensor_copy(path_flag[0:1, 0:1], q_ps[0:1, 0:1]).then_inc(flag_ready, 1)
            dve.wait_ge(row_step, 3)

            def ctx_variance(g, slots, sums):
                if not is_first(g):
                    dve.wait_ge(ctx_rms, g)
                nc.vector.tensor_scalar(c_var[:, slots], sums, 1.0 / D, EPS_RMS, ALU.mult, ALU.add).then_inc(ctx_var, 1)

            def ctx_norms(g, slots):
                def guess():
                    dve.wait_ge(ctx_root, g + 1)
                    nc.vector.reciprocal(c_r0[:, slots], c_root[:, slots]).then_inc(rms_step, 1)

                def its_square():
                    dve.wait_ge(rms_step, 4 * g + 1)
                    nc.vector.tensor_tensor(c_r0sq[:, slots], c_r0[:, slots], c_r0[:, slots], ALU.mult).then_inc(rms_step, 1)

                def near_one():
                    dve.wait_ge(rms_step, 4 * g + 2)
                    nc.vector.tensor_tensor(c_vr[:, slots], c_r0sq[:, slots], c_var[:, slots], ALU.mult).then_inc(rms_step, 1)

                def correction():
                    dve.wait_ge(rms_step, 4 * g + 3)
                    nc.vector.tensor_scalar(c_fix[:, slots], c_vr[:, slots], -0.5, 1.5, ALU.mult, ALU.add).then_inc(rms_step, 1)

                def corrected():
                    dve.wait_ge(rms_step, 4 * g + 4)
                    nc.vector.tensor_tensor(c_rms[:, slots], c_r0[:, slots], c_fix[:, slots], ALU.mult).then_inc(ctx_rms, 1)

                return guess, its_square, near_one, correction, corrected

            def ctx_low(path, u, slot):
                dve.wait_ge(cT_high, path.moved(u) + 1)
                nc.vector.tensor_tensor(cT_hl[:, 1, :, :].rearrange("p k r -> p (k r)"), cT[:, slot, :],
                                        cT_hl[:, 0, :, :].rearrange("p k r -> p (k r)").bitcast(F32),
                                        ALU.subtract).then_inc(cT_split, 1)

            def first_columns_low(j):
                dve.wait_ge(first_cT_high, j + 1)
                nc.vector.tensor_tensor(
                    first_hl[:, 1, j, :, :].rearrange("p k (h r) -> p k h r", h=2),
                    first_cT[:, :, j:j + BLK].unsqueeze(2).to_broadcast([P, KC, 2, BLK]),
                    first_hl[:, 0, j, :, :].rearrange("p k (h r) -> p k h r", h=2).bitcast(F32),
                    ALU.subtract).then_inc(first_cT_split, 1)

            def first_table_low(j):
                dve.wait_ge(*((hi_ready, 1) if j == WIN - 1 else (first_high, j + 1)))
                return nc.vector.scalar_tensor_tensor(
                    table[BLK:P, 0, j, :], first_banks[j][BLK:P, :], first_rms[BLK:P, j:j + 1],
                    table[BLK:P, 0, j, :].bitcast(F32), ALU.mult, ALU.subtract)

            def kv_low(u, slot):
                dve.wait_ge(hi_ready, u + 1)
                nc.vector.scalar_tensor_tensor(kv_lo[:, :], kv_ps[0:ROWS, :], c_rms[:, :].unsqueeze(2)[:, slot, :],
                                               kv_hi[:, :].bitcast(F32), ALU.mult, ALU.subtract).then_inc(lo_ready, 1)

            def make_onehots(path, t):
                if not is_first(t):
                    dve.wait_ge(v_ready, t)
                for c, blk in enumerate(path.blocks):
                    last = nc.vector.tensor_scalar(onehot[:, c, :], idx_tiles[:, t, :], float(BLK * blk), row_of[:, :],
                                                   ALU.subtract, ALU.is_equal)
                last.then_inc(onehot_ready, 1)

            def attention_low(t, i, bank=a_ps):
                dve.wait_ge(aT_high, t + 1)
                nc.vector.tensor_tensor(aT_hl[:, i % 2, 1, :, :].rearrange("p k t -> p (k t)"), bank[:, 0:D],
                                        aT_hl[:, i % 2, 0, :, :].rearrange("p k t -> p (k t)").bitcast(F32),
                                        ALU.subtract).then_inc(aT_split, 1)

            def residual(t):
                dve.wait_ge(o_ready, t + 1)
                nc.vector.tensor_tensor(x_sb[:, t, :], o_bank(t)[:, 0:D], x_sb[:, t, :], ALU.add).then_inc(end_ready, 1)

            def weights(b, i):
                pair = 2 * b + i // 2 - 1
                t = TPB * b + i
                at = (i - 2) % TPB
                both = slice(at, at + 2)

                def square():
                    dve.wait_ge(score_ready, t)
                    nc.vector.scalar_tensor_tensor(w_raw[:, :, :], score[:, both, :], 0.0, score[:, both, :],
                                                   ALU.max, ALU.mult).then_inc(squared_ready, 1)

                def sums():
                    dve.wait_ge(squared_ready, pair + 1)
                    nc.vector.tensor_reduce(den[:, :, :], w_raw[:, :, :].rearrange("p t (j h) -> p t h j", j=WIN),
                                            AX.X, ALU.add).then_inc(den_step, 1)

                def bound():
                    dve.wait_ge(den_step, 3 * pair + 1)
                    dve.wait_ge(x_squared, t)
                    nc.vector.scalar_tensor_tensor(den_max[:, :, :], x_ss[:, both].unsqueeze(2).to_broadcast([P, 2, H]),
                                                   DEN_LEAST, den[:, :, :], ALU.add, ALU.max).then_inc(den_step, 1)

                def invert():
                    dve.wait_ge(den_step, 3 * pair + 2)
                    nc.vector.reciprocal(den_inv[:, :, :], den_max[:, :, :]).then_inc(den_step, 1)

                def normalize():
                    dve.wait_ge(den_step, 3 * pair + 3)
                    nc.vector.tensor_tensor(
                        w_sb[:, both, :].rearrange("p t (j h) -> p t j h", j=WIN),
                        w_raw[:, :, :].rearrange("p t (j h) -> p t j h", j=WIN),
                        den_inv[:, :, :].unsqueeze(2).to_broadcast([P, 2, WIN, H]), ALU.mult).then_inc(w_ready, 1)

                return square, sums, bound, invert, normalize

            def run(path):
                if path.ahead:
                    for j in range(WIN):
                        first_columns_low(j)
                    dve.wait_ge(squares_summed, 1)
                    ctx_variance(0, slice(0, AHEAD), k_win[0:ROWS, 0:AHEAD * P].rearrange("r (u n) -> r u n", n=P)[:, :, 0])
                for k in range(KC):
                    dve.wait_ge(wkv_high, k + 1)
                    nc.vector.scalar_tensor_tensor(wkv_hl[:, 1, k, :], wkv_raw[:, k, :], gkv_sb[:, k:k + 1],
                                                   wkv_hl[:, 0, k, :].bitcast(F32), ALU.mult,
                                                   ALU.subtract).then_inc(wkv_split, 1)
                    if path.ahead and k == 0:
                        for step in ctx_norms(0, slice(0, AHEAD)):
                            step()
                if path.ahead:
                    dve.wait_ge(shifted, 1)
                    nc.vector.tensor_copy(first_rms[:, :], v_win[:, 0:WIN]).then_inc(first_rms_ready, 1)
                    ctx_low(path, 1, 1)
                    first_table_low(0)
                dve.wait_ge(wq_high, 1)
                for k in range(KC):
                    last = nc.vector.scalar_tensor_tensor(wq_hl[:, 1, k, :], wq_raw[:, k, :], gq_sb[:, k:k + 1],
                                                          wq_hl[:, 0, k, :].bitcast(F32), ALU.mult, ALU.subtract)
                last.then_inc(wq_split, 1)
                if path.ahead:
                    first_table_low(1)
                    first_table_low(2).then_inc(lo_ready, 1)

                def body(b):
                    if not path.ahead:
                        dve.wait_ge(ctx_squared, NBLK * (b + 1))
                        ctx_variance(b, slice(0, NBLK), c_ss[:, :])
                        for step in ctx_norms(b, slice(0, NBLK)):
                            step()
                        for u, slot in path.units(b):
                            ctx_low(path, u, slot)
                            kv_low(u, slot)
                        dve.wait_ge(idx_loaded, 16 * (b + 1))
                    for i in range(TPB):
                        t = TPB * b + i
                        steps = norms = [lambda: None] * 5
                        if path.ahead and is_first(b) and i == 2:
                            dve.wait_ge(squares_summed, 2)
                            ctx_variance(1, slice(AHEAD, B), a_ps[0:ROWS, AHEAD:B])
                            norms = ctx_norms(1, slice(AHEAD, B))
                        if i % 2 == 0 and (not is_first(b) or i > 0):
                            steps = weights(b, i)
                        steps[0]()
                        if not is_first(b):
                            attention_low(t - LAG, i)
                        steps[1]()
                        if not path.ahead:
                            make_onehots(path, t)
                        if path.ahead and i == 0 and not is_first(b) and not is_last(b):
                            kv_low(b + 1, b + 1)
                        norms[0]()
                        steps[2]()
                        norms[1]()
                        if makes_table(path, b) and i == first_part(b):
                            ctx_low(path, b + AHEAD, b + AHEAD)
                        steps[3]()
                        norms[2]()
                        dve.wait_ge(q_copied, t + 1)
                        dve.wait_ge(k_ready, t + 1)
                        nc.vector.tensor_tensor(
                            prod[:, i % 2, :].rearrange("p (j d) -> p j d", j=WIN),
                            k_win[:, 0:WIN * D].rearrange("p (j d) -> p j d", j=WIN),
                            q_sb[:, i % 2, :].unsqueeze(1).to_broadcast([P, WIN, D]), ALU.mult).then_inc(prod_ready, 1)
                        steps[4]()
                        norms[3]()
                        if path.ahead and is_first(b) and i == 1:
                            kv_low(1, 1)
                        dve.wait_ge(prod_ready, t + 1)
                        nc.vector.tensor_reduce(score[:, i, :], prod[:, i % 2, :].rearrange("p (a d) -> p a d", d=HD),
                                                AX.X, ALU.add).then_inc(score_ready, 1)
                        norms[4]()

                over_batches(dve, body)
                square, sums, bound, invert, normalize = weights(B, 0)
                square()
                attention_low(NT - 4, 0, a_bank(NT - 4))
                sums()
                bound()
                invert()
                normalize()
                dve.wait_ge(w_ready, 2 * B)
                dve.wait_ge(v_copied, NT - 1)
                weigh(nc.vector, TPB - 2).then_inc(wv_here, 1)
                attention_low(NT - 3, 1, a_bank(NT - 3))
                residual(NT - 4)
                attention_low(NT - 2, 2, a_bank(NT - 2))
                residual(NT - 3)
                attention_low(NT - 1, 3, a_bank(NT - 1))
                residual(NT - 2)
                residual(NT - 1)

            either(dve, run)

        @block.tensor
        def _(pe):
            pe.wait_ge(ones_ready, 1)
            pe.wait_ge(outside_step, 3)
            nc.tensor.matmul(q_ps[0:1, 0:1], outside[:, :], ones[:, 0:1], start=True, stop=True).then_inc(outside_summed, 1)

            def warm(n, to):
                for _ in range(n):
                    nc.tensor.matmul(to[:, 0:P], ones[:, :], ones[:, :], start=True, stop=True)

            warm(WARM, k_win)

            def project(to, columns, weights_hl, which=range(len(PARTS))):
                for n in which:
                    x, y = PARTS[n]
                    for k in range(KC):
                        last = nc.tensor.matmul(to, columns[:, x, k, :], weights_hl[:, y, k, :],
                                                start=(n == 0 and k == 0), stop=(n == len(PARTS) - 1 and k == KC - 1))
                return last

            def kv_products(b, i):
                return [[], [], [0, 1], [2]][i] if is_first(b) else [[0], [1], [2], []][i]

            def kv_project(path, u, which=range(len(PARTS))):
                if 0 in which:
                    pe.wait_ge(cT_split, path.moved(u) + 1)
                    if not is_first(u):
                        pe.wait_ge(lo_ready, u)
                last = project(kv_ps[0:ROWS, :], cT_hl, wkv_hl, which)
                if len(PARTS) - 1 in which:
                    last.then_inc(kv_ready, 1)

            def sum_squares(first, end, group, bank, n=1):
                pe.wait_ge(cT_squared, group + 1)
                for u in range(first, end):
                    for k in range(KC):
                        last = nc.tensor.matmul(bank[0:ROWS, u * n:(u + 1) * n], cT_sq[:, u, k, :], ones[:, 0:n], start=(k == 0),
                                                stop=(k == KC - 1))
                last.then_inc(squares_summed, 1)

            def first_project():
                def products(j, which):
                    for n in which:
                        x, y = PARTS[n]
                        for k in range(KC):
                            last = nc.tensor.matmul(first_banks[j][:, :], first_hl[:, x, j, k, :], wkv_hl[:, y, k, :],
                                                    start=(n == 0 and k == 0),
                                                    stop=(n == len(PARTS) - 1 and k == KC - 1))
                    return last

                pe.wait_ge(wkv_high, KC)
                for j in range(2):
                    pe.wait_ge(first_cT_split, j + 1)
                    products(j, [0, 1])
                pe.wait_ge(ctx_rms, 1)
                pe.wait_ge(shift_ready, 1)
                for j in range(WIN):
                    last = nc.tensor.matmul(v_win[:, j:j + 1], shift[0:ROWS, j, :], c_rms[:, 0:1], start=True, stop=True)
                last.then_inc(shifted, 1)
                pe.wait_ge(wkv_split, KC)
                for j in range(2):
                    products(j, [2]).then_inc(first_ready, 1)
                pe.wait_ge(first_cT_split, WIN)
                products(2, [0, 1, 2]).then_inc(kv_ready, 1)

            def gather(path, b, i, to, at, done):
                n = len(path.blocks)
                for j in range(WIN):
                    for c in range(n):
                        last = nc.tensor.matmul(to[:, j * D:(j + 1) * D], onehot[:, i if path.ahead else c, :],
                                                table[:, b if path.ahead else c, j, at:at + D],
                                                start=(c == 0), stop=(c == n - 1))
                last.then_inc(done, 1)

            def transpose_sum(t, i, to=a_ps):
                if isinstance(t, int) and t == NT - 2:
                    pe.wait_ge(wv_here, 1)
                elif isinstance(t, int) and t == NT - 1:
                    pe.wait_ge(wv_ready, NT - 1)
                else:
                    pe.wait_ge(wv_ready, t + 1)
                for k in range(KC):
                    for j in range(WIN):
                        last = nc.tensor.matmul(to[:, k * P:(k + 1) * P], wv[:, i % 2, j * D + k * P:j * D + (k + 1) * P],
                                                ident[:, :], start=(j == 0), stop=(j == WIN - 1), is_transpose=True)
                last.then_inc(aT_ready, 1)

            def project_out(t, i, to=o_ps):
                pe.wait_ge(aT_split, t + 1)
                if isinstance(t, int) and t >= NT - LAG + 2:
                    pe.wait_ge(end_ready, t - (NT - LAG + 1))
                project(to[:, 0:D], aT_hl[:, i % 2], wo_hl).then_inc(o_ready, 1)

            def run(path):
                if path.ahead:
                    sum_squares(0, AHEAD, 0, k_win, P)
                    first_project()
                pe.wait_ge(wkv_split, KC)
                pe.wait_ge(wq_split, 1)

                def body(b):
                    if not path.ahead:
                        for u, _ in path.units(b):
                            kv_project(path, u)
                    for i in range(TPB):
                        t = TPB * b + i
                        if not is_first(b):
                            transpose_sum(t - LAG, i)
                        pe.wait_ge(xT_split, t + 1)
                        if not first_tile(b, i):
                            pe.wait_ge(q_copied, t)
                        project(q_ps[:, 0:D], xT_hl[:, i], wq_hl).then_inc(q_ready, 1)
                        if path.ahead and first_tile(b, i):
                            pe.wait_ge(lo_ready, 1)
                        elif i == 0:
                            pe.wait_ge(table_loaded, 32 * WIN * path.moved(len(path.blocks) * (b + 1)))
                        pe.wait_ge(onehot_ready, t + 1)
                        if not first_tile(b, i):
                            pe.wait_ge(prod_ready, t)
                        gather(path, b, i, k_win, 0, k_ready)
                        if not first_tile(b, i):
                            pe.wait_ge(v_copied, t)
                        gather(path, b, i, v_win, D, v_ready)
                        if not is_first(b):
                            project_out(t - LAG, i)
                        if path.ahead and first_tile(b, i):
                            kv_project(path, 1)
                        if path.ahead and is_first(b) and i == 1:
                            sum_squares(AHEAD, B, 1, a_ps)
                        if makes_table(path, b) and kv_products(b, i):
                            kv_project(path, b + AHEAD, kv_products(b, i))
                    if is_first(b):
                        pe.wait_ge(wo_split, 1)

                pe.wait_ge(ident_ready, 1)
                over_batches(pe, body)
                pe.wait_ge(q_copied, NT)
                transpose_sum(NT - LAG, 0)
                for t in range(NT - LAG, NT):
                    if t + 1 < NT:
                        transpose_sum(t + 1, t + 1, a_bank(t + 1))
                    project_out(t, t, o_bank(t))

            either(pe, run)


def kernel(x, ctx_1024, itok_BxS_0_255, L0_xattn_gamma_q, L0_xattn_gamma_kv, L0_xattn_Wq, L0_xattn_Wk, L0_xattn_Wv,
           L0_xattn_Wo):
    import numpy as np
    import concourse.bacc as bacc
    from concourse.bass_utils import run_bass_kernel_spmd

    x, ctx, idx = np.asarray(x), np.asarray(ctx_1024), np.asarray(itok_BxS_0_255)
    wq, wk, wv, wo = (np.asarray(w) for w in (L0_xattn_Wq, L0_xattn_Wk, L0_xattn_Wv, L0_xattn_Wo))
    gq, gkv = np.asarray(L0_xattn_gamma_q), np.asarray(L0_xattn_gamma_kv)

    def chunked(a):
        return np.ascontiguousarray(a.reshape(KC, P, -1).transpose(1, 0, 2))

    x_rows = x.reshape(B, P, TPB, D)
    x_cols = x_rows.reshape(B, P, TPB // 2, 2, KC, P).transpose(0, 2, 5, 3, 4, 1)
    idx_cols = idx.reshape(B, P, TPB).transpose(0, 2, 1).reshape(B, S)
    pad = np.zeros((B, BLK + 1, D), ctx.dtype)
    padded = np.concatenate([pad, ctx, pad], axis=1)
    blocks = np.stack([padded[:, c * BLK:c * BLK + ROWS] for c in range(NBLK)], axis=1)
    ctx_cols = blocks.reshape(B, NBLK, ROWS, KC, P).transpose(0, 1, 4, 3, 2)

    arrays = {
        "x_rows": x_rows, "x_cols": x_cols, "ctx_rows": blocks, "ctx_cols": ctx_cols, "idx_cols": idx_cols,
        "idx_all": idx.reshape(P, NT), "gammas": np.stack([gq, gkv]).reshape(2, KC, P).transpose(2, 0, 1),
        "wq": chunked(wq.T), "wkv": chunked(np.concatenate([wk.T, wv.T], axis=1)), "wo": chunked(wo.T),
    }
    arrays = {n: np.ascontiguousarray(a) for n, a in arrays.items()}
    nc = bacc.Bacc("TRN2", target_bir_lowering=False, num_devices=1)
    aps = {n: nc.dram_tensor(n, a.shape, mybir.dt.from_np(a.dtype), kind="ExternalInput").ap() for n, a in arrays.items()}
    out = nc.dram_tensor("out", (B, P, TPB, D), F32, kind="ExternalOutput").ap()
    window_attention(nc, **aps, out=out)
    r = run_bass_kernel_spmd(nc, [arrays], core_ids=[0])
    return r.results[0]["out"].reshape(B, S, D)
```
